# Optimizing a Trainium2 kernel written in Bass

```python
import numpy as np
import jax
import jax.numpy as jnp

def _softmax(x, axis=-1):
    return jax.nn.softmax(x, axis=axis)

def _gelu(x):
    return jax.nn.gelu(x, approximate=True)

def _silu(x):
    return jax.nn.silu(x)

def _sigmoid(x):
    return jax.nn.sigmoid(x)

def _layernorm(x, axis=-1, eps=1e-05):
    m = jnp.mean(x, axis=axis, keepdims=True)
    v = jnp.var(x, axis=axis, keepdims=True)
    return (x - m) / jnp.sqrt(v + eps)

def _scatter_add(tgt, idx, src, axis=0):
    return tgt.at[idx].add(src)

def _segment_sum(src, seg, n):
    return jax.ops.segment_sum(src, seg, n)
kernel_name = 'mk_xattn_ffn_d2_seqx_r8_94a3f3'

def setup_inputs(seed: int=0):
    np.random.seed(seed)
    _w = jnp.asarray

    def _rec_inputs():
        import jax
        import jax.numpy as jnp
        _rk = jax.random.key(seed)
        x = 7.22e-05 + 1 * jax.random.normal(jax.random.fold_in(_rk, 1), (8, 128, 256), jnp.float32)
        _lenS = 128 - jax.random.randint(jax.random.fold_in(_rk, 7), (8,), 0, max(1, 128 // 4) + 1, jnp.int32)
        _lenS2 = 128 - jax.random.randint(jax.random.fold_in(_rk, 8), (8,), 0, max(1, 128 // 4) + 1, jnp.int32)
        _ctx_512P = jax.random.normal(jax.random.fold_in(_rk, 11), (8, 16, 64), jnp.float32)
        _ctx_512c = jax.random.dirichlet(jax.random.fold_in(_rk, 511), 0.3 * jnp.ones((16,), jnp.float32), (8, 128))
        _ctx_512t = jnp.einsum('bsk,bkd->bsd', _ctx_512c, _ctx_512P)
        _ctx_512t = _ctx_512t * jax.lax.rsqrt(jnp.mean(jnp.square(_ctx_512t)) + 1e-12) * 0.953939
        ctx_512 = -0.000514642 + 1.00011 * (_ctx_512t + 0.3 * jax.random.normal(jax.random.fold_in(_rk, 611), (8, 128, 64), jnp.float32))
        return (x, ctx_512)
    x, ctx_512 = _rec_inputs()

    def _L0_xattn_setup():
        import jax, jax.numpy as jnp
        import numpy as np
        B, S, H, NH, L = (2, 256, 256, 16, 64)
        HD = H // NH
        key = jax.random.key(seed)
        k1, k2, k3, k4, k5 = jax.random.split(key, 5)
        scale = 0.02
        return {'q': jax.random.normal(k1, (B, S, H), dtype=jnp.float32), 'latent_kv': jax.random.normal(k2, (B, S, L), dtype=jnp.float32), 'Wq': jax.random.normal(k3, (H, H), dtype=jnp.float32) * scale, 'Wkv_expand': jax.random.normal(k4, (2 * H, L), dtype=jnp.float32) * scale, 'Wout': jax.random.normal(k5, (H, H), dtype=jnp.float32) * scale}
    _L0_xattn_all = _L0_xattn_setup()
    _L0_xattn_in = {k: v for k, v in _L0_xattn_all.items() if k in ('Wq', 'Wkv_expand', 'Wout')}
    del _L0_xattn_all

    def _L0_ffn_setup():
        import jax, jax.numpy as jnp
        import numpy as np
        TOP_K = 2

        def moe_forward(x, w_gate_router, w_gate_proj, w_up_proj, w_down_proj):
            E = w_gate_router.shape[0]
            scores = jnp.einsum('bsd,ed->bse', x, w_gate_router)
            topk_scores, topk_idx = jax.lax.top_k(scores, TOP_K)
            topk_probs = jax.nn.softmax(topk_scores, axis=-1)
            weights = jnp.sum(topk_probs[..., None] * jax.nn.one_hot(topk_idx, E, dtype=x.dtype), axis=-2)
            gate = jnp.einsum('bsd,efd->bsef', x, w_gate_proj)
            up = jnp.einsum('bsd,efd->bsef', x, w_up_proj)
            hidden = jax.nn.silu(gate) * up
            out = jnp.einsum('bsef,edf,bse->bsd', hidden, w_down_proj, weights)
            return out
        key = jax.random.key(seed)
        k1, k2, k3, k4, k5 = jax.random.split(key, 5)
        B, S, D, E, F = (2, 128, 256, 8, 96)
        scale_in = 1.0 / np.sqrt(D)
        scale_ff = 1.0 / np.sqrt(F)
        return {'x': jax.random.normal(k1, (B, S, D), dtype=jnp.float32), 'w_gate_router': jax.random.normal(k2, (E, D), dtype=jnp.float32) * scale_in, 'w_gate_proj': jax.random.normal(k3, (E, F, D), dtype=jnp.float32) * scale_in, 'w_up_proj': jax.random.normal(k4, (E, F, D), dtype=jnp.float32) * scale_in, 'w_down_proj': jax.random.normal(k5, (E, D, F), dtype=jnp.float32) * scale_ff}
    _L0_ffn_all = _L0_ffn_setup()
    _L0_ffn_in = {k: v for k, v in _L0_ffn_all.items() if k in ('w_gate_router', 'w_gate_proj', 'w_up_proj', 'w_down_proj')}
    del _L0_ffn_all

    def _L1_xattn_setup():
        import jax, jax.numpy as jnp
        import numpy as np
        import math
        NUM_Q_HEADS = 32
        NUM_KV_HEADS = 8
        key = jax.random.key(seed)
        k1, k2, k3 = jax.random.split(key, 3)
        B, S, E = (2, 256, 256)
        kv_E = NUM_KV_HEADS * (E // NUM_Q_HEADS)
        q = jax.random.normal(k1, (B, S, E), dtype=jnp.float32)
        k = jax.random.normal(k2, (B, S, kv_E), dtype=jnp.float32)
        v = jax.random.normal(k3, (B, S, kv_E), dtype=jnp.float32)
        return {'q': q, 'k': k, 'v': v}
    _L1_xattn_all = _L1_xattn_setup()
    _L1_xattn_in = {k: v for k, v in _L1_xattn_all.items() if k in ()}
    del _L1_xattn_all

    def _L1_ffn_setup():
        import jax, jax.numpy as jnp
        import numpy as np
        BLOCK = 64

        def dequant4bit(q, scale):
            return (q.astype(jnp.float32) - 7.5) * jnp.repeat(scale, BLOCK, axis=1)
        key = jax.random.key(seed)
        ks = jax.random.split(key, 11)
        B, S, D, H, R = (4, 256, 256, 1024, 16)
        return {'x1': jax.random.normal(ks[0], (B, S, D), jnp.float32), 'w_up_q': jax.random.randint(ks[1], (H, D), 0, 16, dtype=jnp.int32), 'w_up_scale': jax.random.uniform(ks[2], (H, D // BLOCK), jnp.float32) * 0.02, 'b_up': jax.random.normal(ks[3], (H,), jnp.float32) * 0.01, 'w_up_lora_a': jax.random.normal(ks[4], (D, R), jnp.float32) * 0.02, 'w_up_lora_b': jax.random.normal(ks[5], (R, H), jnp.float32) * 0.02, 'w_down_q': jax.random.randint(ks[6], (D, H), 0, 16, dtype=jnp.int32), 'w_down_scale': jax.random.uniform(ks[7], (D, H // BLOCK), jnp.float32) * 0.02, 'b_down': jax.random.normal(ks[8], (D,), jnp.float32) * 0.01, 'w_down_lora_a': jax.random.normal(ks[9], (H, R), jnp.float32) * 0.02, 'w_down_lora_b': jax.random.normal(ks[10], (R, D), jnp.float32) * 0.02}
    _L1_ffn_all = _L1_ffn_setup()
    _L1_ffn_in = {k: v for k, v in _L1_ffn_all.items() if k in ('w_up_q', 'w_up_scale', 'b_up', 'w_up_lora_a', 'w_up_lora_b', 'w_down_q', 'w_down_scale', 'b_down', 'w_down_lora_a', 'w_down_lora_b')}
    del _L1_ffn_all
    return {'x': x, 'ctx_512': ctx_512, 'L0_xattn_Wq': _L0_xattn_in['Wq'], 'L0_xattn_Wkv_expand': _L0_xattn_in['Wkv_expand'], 'L0_xattn_Wout': _L0_xattn_in['Wout'], 'L0_ffn_w_gate_router': _L0_ffn_in['w_gate_router'], 'L0_ffn_w_gate_proj': _L0_ffn_in['w_gate_proj'], 'L0_ffn_w_up_proj': _L0_ffn_in['w_up_proj'], 'L0_ffn_w_down_proj': _L0_ffn_in['w_down_proj'], 'L1_ffn_w_up_q': _L1_ffn_in['w_up_q'], 'L1_ffn_w_up_scale': _L1_ffn_in['w_up_scale'], 'L1_ffn_b_up': _L1_ffn_in['b_up'], 'L1_ffn_w_up_lora_a': _L1_ffn_in['w_up_lora_a'], 'L1_ffn_w_up_lora_b': _L1_ffn_in['w_up_lora_b'], 'L1_ffn_w_down_q': _L1_ffn_in['w_down_q'], 'L1_ffn_w_down_scale': _L1_ffn_in['w_down_scale'], 'L1_ffn_b_down': _L1_ffn_in['b_down'], 'L1_ffn_w_down_lora_a': _L1_ffn_in['w_down_lora_a'], 'L1_ffn_w_down_lora_b': _L1_ffn_in['w_down_lora_b']}

def reference(x, ctx_512, L0_xattn_Wq, L0_xattn_Wkv_expand, L0_xattn_Wout, L0_ffn_w_gate_router, L0_ffn_w_gate_proj, L0_ffn_w_up_proj, L0_ffn_w_down_proj, L1_ffn_w_up_q, L1_ffn_w_up_scale, L1_ffn_b_up, L1_ffn_w_up_lora_a, L1_ffn_w_up_lora_b, L1_ffn_w_down_q, L1_ffn_w_down_scale, L1_ffn_b_down, L1_ffn_w_down_lora_a, L1_ffn_w_down_lora_b):
    import jax
    import jax.numpy as jnp

    def _L0_xattn_ref(q, latent_kv, Wq, Wkv_expand, Wout):
        import jax, jax.numpy as jnp
        import numpy as np
        B, S, H, NH, L = (2, 256, 256, 16, 64)
        HD = H // NH
        b, sq, _ = q.shape
        sk = latent_kv.shape[1]
        qp = q @ Wq.T
        kv = latent_kv @ Wkv_expand.T
        k, v = jnp.split(kv, 2, axis=-1)
        qh = qp.reshape(b, sq, NH, HD).transpose(0, 2, 1, 3)
        kh = k.reshape(b, sk, NH, HD).transpose(0, 2, 1, 3)
        vh = v.reshape(b, sk, NH, HD).transpose(0, 2, 1, 3)
        inv_sqrt_d = 1.0 / jnp.sqrt(jnp.float32(HD))
        scores = jnp.einsum('bhqd,bhkd->bhqk', qh, kh) * inv_sqrt_d
        causal = jnp.tril(jnp.ones((sq, sk), dtype=bool))
        scores = jnp.where(causal, scores, jnp.finfo(scores.dtype).min)
        attn = jax.nn.softmax(scores, axis=-1)
        out = jnp.einsum('bhqk,bhkd->bhqd', attn, vh)
        out = out.transpose(0, 2, 1, 3).reshape(b, sq, H)
        return out @ Wout.T

    def _L0_ffn_ref(x, w_gate_router, w_gate_proj, w_up_proj, w_down_proj):
        import jax, jax.numpy as jnp
        import numpy as np
        TOP_K = 2

        def moe_forward(x, w_gate_router, w_gate_proj, w_up_proj, w_down_proj):
            E = w_gate_router.shape[0]
            scores = jnp.einsum('bsd,ed->bse', x, w_gate_router)
            topk_scores, topk_idx = jax.lax.top_k(scores, TOP_K)
            topk_probs = jax.nn.softmax(topk_scores, axis=-1)
            weights = jnp.sum(topk_probs[..., None] * jax.nn.one_hot(topk_idx, E, dtype=x.dtype), axis=-2)
            gate = jnp.einsum('bsd,efd->bsef', x, w_gate_proj)
            up = jnp.einsum('bsd,efd->bsef', x, w_up_proj)
            hidden = jax.nn.silu(gate) * up
            out = jnp.einsum('bsef,edf,bse->bsd', hidden, w_down_proj, weights)
            return out
        return moe_forward(x, w_gate_router, w_gate_proj, w_up_proj, w_down_proj)

    def _L1_xattn_ref(q, k, v):
        import jax, jax.numpy as jnp
        import numpy as np
        import math
        NUM_Q_HEADS = 32
        NUM_KV_HEADS = 8
        B, S, E = q.shape
        H, KV = (NUM_Q_HEADS, NUM_KV_HEADS)
        D = E // H
        G = H // KV
        scale = math.sqrt(D)
        qh = q.reshape(B, S, KV, G, D).transpose(0, 2, 3, 1, 4)
        kh = k.reshape(B, S, KV, D).transpose(0, 2, 1, 3)
        vh = v.reshape(B, S, KV, D).transpose(0, 2, 1, 3)
        scores = jnp.einsum('bkgsd,bktd->bkgst', qh, kh) / scale
        weights = jax.nn.softmax(scores, axis=-1)
        out = jnp.einsum('bkgst,bktd->bkgsd', weights, vh)
        return out.transpose(0, 3, 1, 2, 4).reshape(B, S, E)

    def _L1_ffn_ref(x1, w_up_q, w_up_scale, b_up, w_up_lora_a, w_up_lora_b, w_down_q, w_down_scale, b_down, w_down_lora_a, w_down_lora_b):
        import jax, jax.numpy as jnp
        import numpy as np
        BLOCK = 64

        def dequant4bit(q, scale):
            return (q.astype(jnp.float32) - 7.5) * jnp.repeat(scale, BLOCK, axis=1)
        w_up = dequant4bit(w_up_q, w_up_scale).T
        y1 = x1 @ w_up + b_up + x1 @ w_up_lora_a @ w_up_lora_b
        x2 = jax.nn.relu(y1)
        w_down = dequant4bit(w_down_q, w_down_scale).T
        y2 = x2 @ w_down + b_down + x2 @ w_down_lora_a @ w_down_lora_b
        return y2
    x = x + _L0_xattn_ref(_layernorm(x, axis=-1), ctx_512, L0_xattn_Wq, L0_xattn_Wkv_expand, L0_xattn_Wout)
    x = x + _L0_ffn_ref(_layernorm(x, axis=-1), L0_ffn_w_gate_router, L0_ffn_w_gate_proj, L0_ffn_w_up_proj, L0_ffn_w_down_proj)
    x = x + _L1_xattn_ref(_layernorm(x, axis=-1), ctx_512, ctx_512)
    x = x + _L1_ffn_ref(_layernorm(x, axis=-1), L1_ffn_w_up_q, L1_ffn_w_up_scale, L1_ffn_b_up, L1_ffn_w_up_lora_a, L1_ffn_w_up_lora_b, L1_ffn_w_down_q, L1_ffn_w_down_scale, L1_ffn_b_down, L1_ffn_w_down_lora_a, L1_ffn_w_down_lora_b)
    return x

_drawn_inputs = setup_inputs


def setup_inputs(seed=0):
    import zlib

    import numpy as np

    out = dict(_drawn_inputs(seed))
    spreads = {}
    factors = {'L0_xattn_Wq': 26.823,
     'L1_ffn_b_up': 8.0,
     'L1_ffn_w_up_lora_a': 3.33,
     'L1_ffn_w_up_lora_b': 3.316,
     'L1_ffn_b_down': 8.0,
     'L1_ffn_w_down_lora_a': 3.366,
     'L1_ffn_w_down_lora_b': 3.505}
    for name, (base, spread) in spreads.items():
        noise = np.random.default_rng([zlib.crc32(name.encode()), seed]).standard_normal(out[name].shape)
        drawn = base * np.exp(spread * noise) if base else spread * noise
        out[name] = jnp.asarray(drawn.astype(out[name].dtype))
    for name, factor in factors.items():
        out[name] = (out[name] * factor).astype(out[name].dtype)
    return out
```

```python
from contextlib import ExitStack

import concourse.bass as bass
from concourse import mybir

F32 = mybir.dt.float32
BF16 = mybir.dt.bfloat16
I32 = mybir.dt.int32
U32 = mybir.dt.uint32
ALU = mybir.AluOpType
ACT = mybir.ActivationFunctionType
AX_X = mybir.AxisListType.X

P = 128
D = 256
DC = D // P
L = 64
NH0, HD0 = 16, 16
NH1, KV1, HD1 = 32, 8, 8
G1 = NH1 // KV1
E, F = 8, 96
FT = E * F // P
H = 1024
HT = H // P
R = 16
BLOCK = 64
W0 = NH0 * (HD0 + 1)
W1 = NH1 * (HD1 + 1)
EPS = 1e-5
MASKED = -1e30
TERMS = 6

Q_PARTS = {"h": (0, 3), "m": (3, 5), "l": (5, 6)}


def build(nc, x, ctx, wq, wkv, wout, wr, wg, wu, wd, upq, ups, bup, upa, upb, dnq, dns, bdn, dna, dnb, out):
    B = x.shape[0]
    PAIRS = B // 2
    PAR = range(2)

    work = [("ct", p) for p in PAR] + [("kv", p) for p in PAR]
    work += [k for p in PAR for k in (("kt1", p), ("kt0", p, 0), ("kt0", p, 1))]
    work += [("xt0", p) for p in PAR] + [("q0", p) for p in PAR]
    work += [("qt0", p, c) for p in PAR for c in range(2)]
    work += [("mt0", p) for p in PAR] + [("aot", p) for p in PAR] + [("o0", p) for p in PAR]
    work += [("xtm", p) for p in PAR] + [("rt", p) for p in PAR] + [("gu", 0), ("gu", 1)]
    work += [("wt", p) for p in PAR] + [("gu", 2)] + [("wb", k) for k in range(FT // 2)]
    work += [("gu", t) for t in range(3, FT)] + [("dn", p) for p in PAR]
    work += [("qt1", p, c) for p in PAR for c in range(2)] + [("mt1", p) for p in PAR]
    work += [("xtf", p) for p in PAR] + [("up", t) for t in range(HT // 2)] + [("fd", p) for p in PAR]
    NW = 3
    uses = [len(work[b::NW]) for b in range(NW)]
    VSTEPS = 38
    scores = [(0, p, t) for p in PAR for t in range(NH0 // 4)] + [(1, p, t) for p in PAR for t in range(NH1 // 4)]
    NS = len(scores)
    NPT = 4

    with ExitStack() as stack:
        def sb(name, shape, dt=F32):
            return stack.enter_context(nc.sbuf_tensor(name, shape, dt))

        def psum(name, shape, dt=F32):
            return stack.enter_context(nc.psum_tensor(name, shape, dt))

        def sem(name):
            return stack.enter_context(nc.semaphore(name))

        def sems(name, n=2):
            return [sem(f"{name}{k}") for k in range(n)]

        def pair(name, shape, dt=F32):
            return [sb(f"{name}{p}", shape, dt) for p in PAR]

        wq_sb = sb("wq_sb", [P, DC, D])
        wkv_sb = sb("wkv_sb", [L, 2 * D])
        wout_sb = sb("wout_sb", [P, DC, D])
        wr_sb = sb("wr_sb", [P, DC, E])
        wg_sb = sb("wg_sb", [P, DC, E * F])
        wu_sb = sb("wu_sb", [P, DC, E * F])
        wd_sb = sb("wd_sb", [P, FT, D])
        upq_sb = sb("upq_sb", [P, DC, H], I32)
        dnq_sb = sb("dnq_sb", [P, HT, D], I32)
        ups_sb = sb("ups_sb", [P, DC, H])
        dns_sb = sb("dns_sb", [P, HT, D])
        upw = sb("upw", [P, DC, H])
        dnw = sb("dnw", [P, HT, D])
        bup_sb = sb("bup_sb", [P, HT])
        bdn_sb = sb("bdn_sb", [P, D])
        upa_sb = sb("upa_sb", [R, D])
        upb_sb = sb("upb_sb", [R, H])
        dna_sb = sb("dna_sb", [R, H])
        dnb_sb = sb("dnb_sb", [R, D])
        idf = sb("idf", [P, P])
        idb = sb("idb", [P, P], BF16)
        maskq = sb("maskq", [P, 4, P], BF16)
        maskk = sb("maskk", [P, 4, P], BF16)
        selg = sb("selg", [P, KV1, P], BF16)
        sele = sb("sele", [P, E, F], BF16)
        mhalf = sb("mhalf", [P, 1])
        expert = sb("expert", [P, E])
        xin = pair("xin", [P, D])
        cin = pair("cin", [P, L])
        ct = pair("ct", [L, P])
        kres = pair("kres", [P, D])
        kexp0 = pair("kexp0", [P, NH0, P], BF16)
        kt0 = pair("kt0", [P, NH0, P], BF16)
        va0 = pair("va0", [P, NH0, HD0 + 1])
        kres1 = pair("kres1", [P, L])
        kexp1 = pair("kexp1", [P, KV1, L], BF16)
        kz1 = pair("kz1", [P, KV1, P], BF16)
        va1 = pair("va1", [P, KV1, HD1 + 1])
        stats = pair("stats", [P, 6])
        mv = pair("mv", [P, 2])
        var_eps = pair("var_eps", [P, 1])
        rstd = pair("rstd", [P, 1])
        xhat = pair("xhat", [P, D])
        xht = [sb(f"xht{p}", [P, DC, P]) for p in PAR]
        qres = pair("qres", [P, D])
        qexp0 = pair("qexp0", [P, NH0, P], BF16)
        qexp1 = pair("qexp1", [P, NH1, L], BF16)
        qt0 = pair("qt0", [P, NH0, P], BF16)
        qt1 = pair("qt1", [P, NH1 // 2, P], BF16)
        nmax = pair("nmax", [P, G1, KV1])
        mexp0 = pair("mexp0", [P, G1, P], BF16)
        mexp1 = pair("mexp1", [P, G1, P], BF16)
        mt = pair("mt", [P, G1 * P], BF16)
        pt = [sb(f"pt{k}", [P, 4, P]) for k in range(NPT)]
        rden = pair("rden", [P, NH1])
        ao = pair("ao", [P, D])
        aot = pair("aot", [P, DC, P])
        x1 = pair("x1", [P, D])
        x2 = pair("x2", [P, D])
        x3 = pair("x3", [P, D])
        xb = pair("xb", [P, D])
        xo = pair("xo", [P, D])
        xmt = sb("xmt", [P, DC, 2 * P])
        xft = sb("xft", [P, DC, 2 * P])
        top8 = pair("top8", [P, 8])
        idx8 = pair("idx8", [P, 8], U32)
        idxf = pair("idxf", [P, 2])
        score = pair("score", [P, E])
        gap = pair("gap", [P, 1])
        egap = pair("egap", [P, 1])
        den2 = pair("den2", [P, 1])
        p12 = pair("p12", [P, 2])
        w1st = pair("w1st", [P, E])
        w2nd = pair("w2nd", [P, E])
        wtok = pair("wtok", [P, E])
        wres = pair("wres", [P, E])
        wexp = pair("wexp", [P, P], BF16)
        wt = sb("wt", [P, 2 * P], BF16)
        wb = sb("wb", [P, FT, 2 * P])
        th = [sb(f"th{k}", [P, 2 * P]) for k in range(2)]
        sg = [sb(f"sg{k}", [P, 2 * P]) for k in range(2)]
        su = [sb(f"su{k}", [P, 2 * P]) for k in range(2)]
        hid = wb
        hft = ups_sb[:].rearrange("p c (h n) -> p (c h) n", n=2 * P)

        ps_nat = [psum(f"ps_nat{k}", [P, 512]) for k in range(2)]
        ps_tr = [psum(f"ps_tr{k}", [P, 512]) for k in range(2)]
        ps_pv = psum("ps_pv", [P, 512])
        ps_w = [psum(f"ps_w{k}", [P, 512]) for k in range(NW)]
        all_banks = ps_nat + ps_tr + [ps_pv] + ps_w

        x_in, c_in = sems("x_in"), sems("c_in")
        ld_kq, ld_out, ld_moe, ld_down, ld_lora, ld_ffn = (sem(f"ld_{n}") for n in
                                                           ("kq", "out", "moe", "down", "lora", "ffn"))
        stored = sems("stored")
        pool_set, const_ready, kexp1_zeroed = sem("pool_set"), sem("const_ready"), sem("kexp1_zeroed")
        lora_mm, lora_copied = sem("lora_mm"), sem("lora_copied")
        deq_tmp, deq_ready = sem("deq_tmp"), sem("deq_ready")
        w_full, w_read = sem("w_full"), sems("w_read", NW)
        nat_full, max_ready = sem("nat_full"), sem("max_ready")
        tr_full, exp_ready = sem("tr_full"), sem("exp_ready")
        pv_done, ao_ready = sem("pv_done"), sem("ao_ready")
        ln_var, ln_pool, ln_rstd, xhat_ready = sems("ln_var"), sems("ln_pool"), sems("ln_rstd"), sems("xhat_ready")
        v0_ready, kh0_ready, km0_ready, kexp0_ready = sems("v0_ready"), sems("kh0_ready"), sems("km0_ready"), sems("kexp0_ready")
        v1_ready, kh1_ready, kres1_ready, km1_ready, kexp1_ready = (sems(n) for n in (
            "v1_ready", "kh1_ready", "kres1_ready", "km1_ready", "kexp1_ready"))
        qh_ready, qres_ready, qm_ready, qexp_ready = sems("qh_ready"), sems("qres_ready"), sems("qm_ready"), sems("qexp_ready")
        mexp_ready = sems("mexp_ready")
        x3_ready, xb_ready = sems("x3_ready"), sems("xb_ready")
        gap_ready, egap_ready, wexp_ready = sems("gap_ready"), sems("egap_ready"), sems("wexp_ready")
        th_ready, sg_ready, hid_ready = sem("th_ready"), sem("sg_ready"), sem("hid_ready")
        vstep = sem("vstep")

        block = stack.enter_context(nc.Block())
        LD_FFN = 16 * 10
        N_CONST = 2 * 7 + 4 + 9

        def wait_at_least(eng, s, count):
            if not isinstance(count, int) or count > 0:
                eng.wait_ge(s, count)

        def detach(eng):
            eng.nop(nofuse=True)

        def work_sem(key):
            return w_read[work.index(key) % NW]

        def work_bank(key):
            return ps_w[work.index(key) % NW]

        def wait_free(eng, key, i):
            n = work.index(key)
            wait_at_least(eng, w_read[n % NW], i * uses[n % NW] + n // NW)

        def wait_full(eng, key, i):
            eng.wait_ge(w_full, i * len(work) + work.index(key) + 1)

        def wait_read(eng, key, i):
            n = work.index(key)
            eng.wait_ge(w_read[n % NW], i * uses[n % NW] + n // NW + 1)

        def iterations(eng, body, after_first=None):
            body(0)
            if after_first:
                after_first()
            with eng.Fori(1, PAIRS) as i:
                body(i)

        def heads(ap, hd):
            return ap.rearrange("p (h d) -> p h d", d=hd)

        def slots(exp, hd):
            return exp[:, :, 0:TERMS * hd].rearrange("p h (s d) -> p h s d", d=hd)

        def repeated(ap, n, hd):
            h = ap.shape[1] // hd
            return ap.rearrange("p (h s d) -> p h s d", s=1, d=hd).broadcast_to([P, h, n, hd])

        @block.sync
        def _(sp):
            def load(i):
                for p in PAR:
                    wait_at_least(sp, w_full, i * len(work))
                    wait_at_least(sp, kexp1_ready[p], i)
                    sp.dma_start(cin[p][:], ctx[bass.ds(2 * i + p, 1), :, :].rearrange("a t c -> t (a c)")).then_inc(c_in[p], 16)
                    if not isinstance(i, int):
                        wait_read(sp, ("o0", p), i - 1)
                    sp.dma_start(xin[p][:], x[bass.ds(2 * i + p, 1), :, :].rearrange("a t c -> t (a c)")).then_inc(x_in[p], 16)

            def store(i):
                for p in PAR:
                    wait_read(sp, ("fd", p), i)
                    sp.dma_start(out[bass.ds(2 * i + p, 1), :, :].rearrange("a t c -> t (a c)"), xo[p][:]).then_inc(stored[p], 16)

            load(0)
            sp.dma_start(wkv_sb[:], wkv).then_inc(ld_kq, 16)
            sp.dma_start(wq_sb[:], wq.rearrange("(c p) n -> p c n", p=P)).then_inc(ld_kq, 16)
            sp.dma_start(wout_sb[:], wout.rearrange("(c p) n -> p c n", p=P)).then_inc(ld_out, 16)
            sp.dma_start(wr_sb[:], wr.rearrange("(c p) n -> p c n", p=P)).then_inc(ld_moe, 16)
            sp.dma_start(wg_sb[:], wg.rearrange("(c p) n -> p c n", p=P)).then_inc(ld_moe, 16)
            sp.dma_start(wu_sb[:], wu.rearrange("(c p) n -> p c n", p=P)).then_inc(ld_moe, 16)
            sp.dma_start(wd_sb[:], wd.rearrange("(c p) n -> p c n", p=P)).then_inc(ld_down, 16)
            for c in range(DC):
                for half in range(2):
                    sp.dma_start(ups_sb[half * BLOCK:(half + 1) * BLOCK, c, :],
                                 ups[2 * c + half:2 * c + half + 1, :].broadcast_to([BLOCK, H])).then_inc(ld_ffn, 16)
            for half in range(2):
                sp.dma_start(dns_sb[half * BLOCK:(half + 1) * BLOCK, :, :],
                             dns.rearrange("(c a) n -> a c n", a=2)[half:half + 1, :, :].broadcast_to([BLOCK, HT, D])).then_inc(ld_ffn, 16)
            sp.dma_start(upq_sb[:], upq.rearrange("(c p) n -> p c n", p=P)).then_inc(ld_ffn, 16)
            sp.dma_start(dnq_sb[:], dnq.rearrange("(c p) n -> p c n", p=P)).then_inc(ld_ffn, 16)
            sp.dma_start(bup_sb[:], bup).then_inc(ld_ffn, 16)
            sp.dma_start(bdn_sb[:], bdn.broadcast_to([P, D])).then_inc(ld_ffn, 16)
            with sp.Fori(1, PAIRS) as i:
                load(i)
                store(i - 1)
            store(PAIRS - 1)
            for p in PAR:
                sp.wait_ge(stored[p], 16 * PAIRS)


        @block.gpsimd
        def _(pool):
            g = nc.gpsimd
            zeroed = [idf, idb, maskq, maskk, selg, sele]
            for t in zeroed:
                g.memset(t[:], 0.0).then_inc(pool_set, 1)
            g.memset(mhalf[:], -0.5).then_inc(pool_set, 1)
            pool.wait_ge(pool_set, len(zeroed) + 1)

            def fill(t, value, pattern, base, cm, op=ALU.not_equal):
                g.affine_select(out=t, in_=t, compare_op=op, fill=value, base=base, pattern=pattern,
                                channel_multiplier=cm).then_inc(const_ready, 1)

            fill(idf[:], 1.0, [[-1, P]], 0, 1)
            fill(idb[:], 1.0, [[-1, P]], 0, 1)
            fill(maskq[:], MASKED, [[0, 4], [-1, P]], 0, 1, ALU.is_ge)
            fill(maskk[:], MASKED, [[0, 4], [1, P]], 0, -1, ALU.is_ge)
            fill(selg[:], 1.0, [[-1, KV1], [0, P]], 0, 1)
            fill(sele[:], 0.5, [[-1, E], [0, F]], 0, 1)
            pool.wait_ge(const_ready, 6)
            fill(selg[:], 1.0, [[-1, KV1], [0, P]], -KV1, 1)
            fill(sele[:], 0.5, [[-1, E], [0, F]], -E, 1)
            pool.wait_ge(const_ready, 8)
            fill(sele[:], 0.5, [[-1, E], [0, F]], -2 * E, 1)
            for t in kexp0 + qexp0 + kz1 + qexp1 + mexp0 + mexp1 + wexp:
                g.memset(t[:], 0.0).then_inc(const_ready, 1)
            for t in va0 + va1:
                g.memset(t[:], 1.0).then_inc(const_ready, 1)
            pool.wait_ge(const_ready, N_CONST)

            def layernorm_rstd(i, p, s):
                pool.wait_ge(ln_var[p], 4 * i + s + 1)
                detach(pool)
                g.tensor_scalar(var_eps[p][:], mv[p][:, 1:2], EPS, None, ALU.add).then_inc(ln_pool[p], 1)
                pool.wait_ge(ln_pool[p], 4 * i + s + 1)
                g.tensor_tensor(rstd[p][:], var_eps[p][:], mhalf[:], ALU.pow).then_inc(ln_rstd[p], 1)

            def body(i):
                for p in PAR:
                    layernorm_rstd(i, p, 0)
                for p in PAR:
                    pool.wait_ge(c_in[p], 16 * (i + 1))
                    wait_at_least(pool, pv_done, NS * i)
                    detach(pool)
                    g.tensor_copy(va1[p][:, :, 0:HD1], heads(cin[p][:], HD1)).then_inc(v1_ready[p], 1)
                    pool.wait_ge(kh1_ready[p], i + 1)
                    k1 = slots(kexp1[p], HD1)
                    res = heads(kres1[p][:], HD1)
                    g.tensor_tensor(res, heads(cin[p][:], HD1), k1[:, :, 1, :], ALU.subtract).then_inc(kres1_ready[p], 1)
                    pool.wait_ge(kres1_ready[p], i + 1)
                    detach(pool)
                    g.tensor_copy(k1[:, :, 2:5:2, :], repeated(kres1[p][:], 2, HD1)).then_inc(km1_ready[p], 1)
                    pool.wait_ge(km1_ready[p], i + 1)
                    g.tensor_tensor(k1[:, :, 0, :], res, k1[:, :, 2, :], ALU.subtract).then_inc(kexp1_ready[p], 1)
                for p in PAR:
                    wait_read(pool, ("kv", p), i)
                    k0 = slots(kexp0[p], HD0)
                    detach(pool)
                    g.tensor_copy(k0[:, :, 2:5:2, :], repeated(kres[p][:], 2, HD0)).then_inc(km0_ready[p], 1)
                    pool.wait_ge(km0_ready[p], i + 1)
                    g.tensor_tensor(k0[:, :, 0, :], heads(kres[p][:], HD0), k0[:, :, 2, :], ALU.subtract).then_inc(kexp0_ready[p], 1)

                def query_parts(p, s, qexp, hd):
                    if s == 0:
                        wait_read(pool, ("q0", p), i)
                    else:
                        pool.wait_ge(qres_ready[p], i + 1)
                    q = slots(qexp[p], hd)
                    detach(pool)
                    g.tensor_copy(q[:, :, 3:5, :], repeated(qres[p][:], 2, hd)).then_inc(qm_ready[p], 1)
                    pool.wait_ge(qm_ready[p], 2 * i + s + 1)
                    g.tensor_tensor(q[:, :, 5, :], heads(qres[p][:], hd), q[:, :, 3, :], ALU.subtract).then_inc(qexp_ready[p], 1)

                for p in PAR:
                    query_parts(p, 0, qexp0, HD0)
                for p in PAR:
                    layernorm_rstd(i, p, 1)
                for t in range(FT):
                    wait_read(pool, ("wb", t // 2), i)
                    wait_read(pool, ("gu", t), i)
                    g.tensor_tensor(hid[:, t, :], su[t % 2][:], wb[:, t, :], ALU.mult).then_inc(hid_ready, 1)
                for p in PAR:
                    layernorm_rstd(i, p, 2)
                for p in PAR:
                    query_parts(p, 1, qexp1, HD1)
                for p in PAR:
                    layernorm_rstd(i, p, 3)
                pool.wait_ge(ld_ffn, LD_FFN)
                for p in PAR:
                    pool.wait_ge(x3_ready[p], i + 1)
                    g.tensor_tensor(xb[p][:], x3[p][:], bdn_sb[:], ALU.add).then_inc(xb_ready[p], 1)

            iterations(pool, body)

        @block.scalar
        def _(act):
            a = nc.scalar
            act.dma_start(upa_sb[:], upa).then_inc(ld_lora, 16)
            act.dma_start(upb_sb[:], upb).then_inc(ld_lora, 16)
            act.dma_start(dna_sb[:], dna).then_inc(ld_lora, 16)
            act.dma_start(dnb_sb[:], dnb).then_inc(ld_lora, 16)
            for b in range(4):
                act.wait_ge(lora_mm, b + 1)
                a.activation(upw[:, b // 2, (b % 2) * 512:(b % 2 + 1) * 512], all_banks[b][:], ACT.Copy).then_inc(lora_copied, 1)
            for b in range(4):
                act.wait_ge(lora_mm, 5 + b)
                a.activation(dnw[:, 2 * b:2 * b + 2, :], all_banks[4 + b][:].rearrange("p (c n) -> p c n", c=2), ACT.Copy).then_inc(lora_copied, 1)
            act.wait_ge(const_ready, N_CONST)
            act.wait_ge(kexp1_zeroed, 2)

            def exps(i, layer, p):
                scale = float(HD1 if layer else HD0) ** -0.5
                for t in range((NH1 if layer else NH0) // 4):
                    n = scores.index((layer, p, t))
                    act.wait_ge(tr_full, NS * i + n + 1)
                    if n >= NPT:
                        act.wait_ge(pv_done, NS * i + n - NPT + 1)
                    else:
                        wait_at_least(act, pv_done, NS * i + n - NPT + 1)
                    a.activation(pt[n % NPT][:], ps_tr[n % 2][:].rearrange("p (h q) -> p h q", h=4), ACT.Exp,
                                 scale=scale).then_inc(exp_ready, 1)

            def transposed(key, dst, i):
                wait_full(act, key, i)
                a.activation(dst, work_bank(key)[:, 0:D].rearrange("p (c t) -> p c t", c=DC), ACT.Copy).then_inc(work_sem(key), 1)

            def body(i):
                for p in PAR:
                    act.wait_ge(c_in[p], 16 * (i + 1))
                    a.activation(slots(kexp1[p], HD1)[:, :, 1:6:2, :], repeated(cin[p][:], 3, HD1), ACT.Copy).then_inc(kh1_ready[p], 1)
                for p in PAR:
                    wait_full(act, ("kv", p), i)
                    kv = work_bank(("kv", p))
                    wait_at_least(act, pv_done, NS * i)
                    a.activation(va0[p][:, :, 0:HD0], heads(kv[:, D:2 * D], HD0), ACT.Copy).then_inc(v0_ready[p], 1)
                    a.activation(slots(kexp0[p], HD0)[:, :, 1:6:2, :], repeated(kv[:, 0:D], 3, HD0), ACT.Copy).then_inc(kh0_ready[p], 1)
                for p in PAR:
                    transposed(("xt0", p), xht[p][:], i)
                for p in PAR:
                    wait_full(act, ("q0", p), i)
                    a.activation(slots(qexp0[p], HD0)[:, :, 0:3, :], repeated(work_bank(("q0", p))[:, 0:D], 3, HD0), ACT.Copy).then_inc(qh_ready[p], 1)
                for p in PAR:
                    exps(i, 0, p)
                for p in PAR:
                    transposed(("aot", p), aot[p][:], i)
                for p in PAR:
                    transposed(("xtm", p), xmt[:, :, p * P:(p + 1) * P], i)

                def tanh(t):
                    wait_full(act, ("gu", t), i)
                    wait_at_least(act, sg_ready, FT * i + t - 1)
                    a.activation(th[t % 2][:], work_bank(("gu", t))[:, 0:2 * P], ACT.Tanh, scale=0.5).then_inc(th_ready, 1)

                for p in PAR:
                    act.wait_ge(gap_ready[p], i + 1)
                    a.activation(egap[p][:], gap[p][:], ACT.Exp).then_inc(egap_ready[p], 1)
                for t in range(3):
                    tanh(t)
                for k in range(FT // 2):
                    wait_full(act, ("wb", k), i)
                    a.activation(wb[:, 2 * k:2 * k + 2, :], work_bank(("wb", k))[:].rearrange("p (t n) -> p t n", t=2),
                                 ACT.Copy).then_inc(work_sem(("wb", k)), 1)
                for t in range(3, FT):
                    tanh(t)
                for p in PAR:
                    act.wait_ge(xhat_ready[p], 4 * i + 3)
                    a.activation(slots(qexp1[p], HD1)[:, :, 0:3, :], repeated(xhat[p][:], 3, HD1), ACT.Copy).then_inc(qh_ready[p], 1)
                for p in PAR:
                    exps(i, 1, p)
                for p in PAR:
                    transposed(("xtf", p), xft[:, :, p * P:(p + 1) * P], i)
                act.wait_ge(ld_ffn, LD_FFN)
                for t in range(HT):
                    key = ("up", t // 2)
                    if t % 2 == 0:
                        wait_full(act, key, i)
                    relu = a.activation(hft[:, t, :], work_bank(key)[:, (t % 2) * 2 * P:(t % 2 + 1) * 2 * P], ACT.Relu,
                                        bias=bup_sb[:, t:t + 1])
                    if t % 2 == 1:
                        relu.then_inc(work_sem(key), 1)

            iterations(act, body)

        @block.vector
        def _(dve):
            v = nc.vector
            step = {"i": 0, "k": 0}

            def done(ins):
                step["k"] += 1
                ins.then_inc(vstep, 1)
                dve.wait_ge(vstep, VSTEPS * step["i"] + step["k"])

            def stats_of(i, p, src):
                done(v.bn_stats(stats[p][:], src[p][:]))
                detach(dve)
                v.bn_aggr(mv[p][:], stats[p][:]).then_inc(ln_var[p], 1)

            def normalise(i, p, s, src):
                dve.wait_ge(ln_rstd[p], 4 * i + s + 1)
                v.tensor_scalar(xhat[p][:], src[p][:], mv[p][:, 0:1], rstd[p][:], ALU.subtract, ALU.mult).then_inc(xhat_ready[p], 1)

            def query_rest(i, p, s, src, qexp, hd):
                dve.wait_ge(qh_ready[p], 2 * i + s + 1)
                return v.tensor_tensor(heads(qres[p][:], hd), heads(src, hd), slots(qexp[p], hd)[:, :, 0, :], ALU.subtract)

            def copy_transposes(i, key, dst):
                wait_full(dve, key, i)
                v.tensor_copy(dst, work_bank(key)[:].bitcast(BF16).rearrange("p (h t) -> p h t", t=P)).then_inc(work_sem(key), 1)

            def maxima(i, layer, p):
                for t in range((NH1 if layer else NH0) // 4):
                    n = scores.index((layer, p, t))
                    dve.wait_ge(nat_full, NS * i + n + 1)
                    bank = ps_nat[n % 2][:]
                    if layer:
                        u, j = t // 2, 2 * (t % 2)
                        src = bank.rearrange("p (j g k) -> p j g k", j=2, g=2)
                        dst = nmax[p][:, j:j + 2, 2 * u:2 * u + 2]
                    else:
                        src = bank.rearrange("p (j k) -> p j k", j=4)
                        dst = nmax[p][:, :, t]
                    v.tensor_reduce(dst, src, AX_X, ALU.max, negate=True).then_inc(max_ready, 1)
                groups = KV1 if layer else NH0 // 4
                n = scores.index((layer, p, 0)) + (NH1 if layer else NH0) // 4
                dve.wait_ge(max_ready, NS * i + n)
                mexp = (mexp1 if layer else mexp0)[p]
                done(v.tensor_copy(mexp[:, :, 0:groups], nmax[p][:, :, 0:groups]))
                v.tensor_tensor(mexp[:, :, KV1:KV1 + groups], nmax[p][:, :, 0:groups], mexp[:, :, 0:groups],
                                ALU.subtract).then_inc(mexp_ready[p], 1)

            def copy_maxima(i, layer, p):
                key = (f"mt{layer}", p)
                wait_full(dve, key, i)
                v.tensor_copy(mt[p][:], work_bank(key)[:, 0:2 * P].bitcast(BF16)).then_inc(work_sem(key), 1)

            def attended(i, layer, p):
                nh, hd = (NH1, HD1) if layer else (NH0, HD0)
                dve.wait_ge(pv_done, NS * i + scores.index((layer, p, 0)) + nh // 4)
                o = ps_pv[:, 0:nh * (hd + 1)].rearrange("p (h d) -> p h d", d=hd + 1)
                r = rden[p][:, 0:nh].rearrange("p (h d) -> p h d", d=1)
                done(v.reciprocal(r, o[:, :, hd:hd + 1]))
                v.tensor_tensor(heads(ao[p][:], hd), o[:, :, 0:hd], r.broadcast_to([P, nh, hd]), ALU.mult).then_inc(ao_ready, 1)

            def router(i, p):
                key = ("rt", p)
                wait_full(dve, key, i)
                v.tensor_copy(score[p][:], work_bank(key)[:, 0:E]).then_inc(work_sem(key), 1)
                wait_read(dve, key, i)
                detach(dve)
                done(v.max(top8[p][:], score[p][:]))
                v.tensor_tensor(gap[p][:], top8[p][:, 1:2], top8[p][:, 0:1], ALU.subtract).then_inc(gap_ready[p], 1)
                detach(dve)
                done(v.max_index(idx8[p][:], top8[p][:], score[p][:]))
                done(v.tensor_copy(idxf[p][:], idx8[p][:, 0:2]))

            def router_weights(i, p):
                dve.wait_ge(egap_ready[p], i + 1)
                done(v.tensor_scalar(den2[p][:], egap[p][:], 1.0, None, ALU.add))
                done(v.reciprocal(p12[p][:, 0:1], den2[p][:]))
                done(v.tensor_tensor(p12[p][:, 1:2], p12[p][:, 0:1], egap[p][:], ALU.mult))
                v.tensor_scalar(w1st[p][:], expert[:], idxf[p][:, 0:1], p12[p][:, 0:1], ALU.is_equal, ALU.mult)
                done(v.tensor_scalar(w2nd[p][:], expert[:], idxf[p][:, 1:2], p12[p][:, 1:2], ALU.is_equal, ALU.mult))
                done(v.tensor_tensor(wtok[p][:], w1st[p][:], w2nd[p][:], ALU.add))
                done(v.tensor_copy(wexp[p][:, 0:E], wtok[p][:]))
                done(v.tensor_tensor(wres[p][:], wtok[p][:], wexp[p][:, 0:E], ALU.subtract))
                done(v.tensor_copy(wexp[p][:, E:2 * E], wres[p][:]))
                v.tensor_tensor(wexp[p][:, 2 * E:3 * E], wres[p][:], wexp[p][:, E:2 * E], ALU.subtract).then_inc(wexp_ready[p], 1)

            def hidden(i, t):
                key = ("gu", t)
                dve.wait_ge(th_ready, FT * i + t + 1)
                v.scalar_tensor_tensor(sg[t % 2][:], th[t % 2][:], 1.0, work_bank(key)[:, 0:2 * P], ALU.add, ALU.mult).then_inc(sg_ready, 1)
                dve.wait_ge(sg_ready, FT * i + t + 1)
                wait_at_least(dve, hid_ready, FT * i + t - 1)
                v.tensor_tensor(su[t % 2][:], sg[t % 2][:], work_bank(key)[:, 2 * P:4 * P], ALU.mult).then_inc(work_sem(key), 1)

            def add_rows(i, key, dst, src):
                wait_full(dve, key, i)
                v.tensor_tensor(dst[:], src[:], work_bank(key)[:, 0:D], ALU.add).then_inc(work_sem(key), 1)
                wait_read(dve, key, i)

            for e in range(E):
                v.memset(expert[:, e:e + 1], float(e))
            v.memset(kexp1[0][:], 0.0).then_inc(kexp1_zeroed, 1)
            v.memset(kexp1[1][:], 0.0).then_inc(kexp1_zeroed, 1)
            dve.wait_ge(const_ready, N_CONST)
            dve.wait_ge(kexp1_zeroed, 2)
            dve.wait_ge(lora_copied, 8)

            def body(i):
                step["i"], step["k"] = i, 0
                for p in PAR:
                    wait_full(dve, ("ct", p), i)
                    v.tensor_copy(ct[p][:], work_bank(("ct", p))[0:L, 0:P]).then_inc(work_sem(("ct", p)), 1)
                for p in PAR:
                    dve.wait_ge(x_in[p], 16 * (i + 1))
                    stats_of(i, p, xin)
                for p in PAR:
                    dve.wait_ge(kh0_ready[p], i + 1)
                    v.tensor_tensor(heads(kres[p][:], HD0), heads(work_bank(("kv", p))[:, 0:D], HD0),
                                    slots(kexp0[p], HD0)[:, :, 1, :], ALU.subtract).then_inc(work_sem(("kv", p)), 1)
                for p in PAR:
                    normalise(i, p, 0, xin)
                for p in PAR:
                    key = ("kt1", p)
                    wait_full(dve, key, i)
                    t = work_bank(key)[:, 0:2 * P].bitcast(BF16).rearrange("p (u t) -> p u t", t=P)
                    for half in range(2):
                        rows = slice(half * L, (half + 1) * L)
                        last = v.tensor_copy(kz1[p][rows, half::2, :], t[rows])
                    last.then_inc(work_sem(key), 1)
                    for c in range(2):
                        copy_transposes(i, ("kt0", p, c), kt0[p][:, 8 * c:8 * c + 8, :])
                for p in PAR:
                    query_rest(i, p, 0, work_bank(("q0", p))[:, 0:D], qexp0, HD0).then_inc(work_sem(("q0", p)), 1)
                for p in PAR:
                    for c in range(2):
                        copy_transposes(i, ("qt0", p, c), qt0[p][:, 8 * c:8 * c + 8, :])
                for p in PAR:
                    maxima(i, 0, p)
                for p in PAR:
                    copy_maxima(i, 0, p)
                for p in PAR:
                    attended(i, 0, p)
                for p in PAR:
                    add_rows(i, ("o0", p), x1[p], xin[p])
                    stats_of(i, p, x1)
                for p in PAR:
                    normalise(i, p, 1, x1)
                for p in PAR:
                    router(i, p)
                for p in PAR:
                    router_weights(i, p)
                hidden(i, 0)
                hidden(i, 1)
                for p in PAR:
                    key = ("wt", p)
                    wait_full(dve, key, i)
                    v.tensor_copy(wt[:, p * P:(p + 1) * P], work_bank(key)[:, 0:P // 2].bitcast(BF16)).then_inc(work_sem(key), 1)
                for t in range(2, FT):
                    hidden(i, t)
                for p in PAR:
                    add_rows(i, ("dn", p), x2[p], x1[p])
                    stats_of(i, p, x2)
                for p in PAR:
                    dve.wait_ge(ln_rstd[p], 4 * i + 3)
                    src = x2[p][:].rearrange("p (u g j d) -> p u g j d", u=KV1 // 2, g=2, j=G1)
                    dst = xhat[p][:].rearrange("p (u j g d) -> p u j g d", u=KV1 // 2, g=2, j=G1)
                    for g in range(2):
                        last = v.tensor_scalar(dst[:, :, :, g, :], src[:, :, g, :, :], mv[p][:, 0:1], rstd[p][:], ALU.subtract, ALU.mult)
                    last.then_inc(xhat_ready[p], 1)
                for p in PAR:
                    dve.wait_ge(xhat_ready[p], 4 * i + 3)
                    query_rest(i, p, 1, xhat[p][:], qexp1, HD1).then_inc(qres_ready[p], 1)
                for p in PAR:
                    for c in range(2):
                        copy_transposes(i, ("qt1", p, c), qt1[p][:, 8 * c:8 * c + 8, :])
                for p in PAR:
                    maxima(i, 1, p)
                for p in PAR:
                    copy_maxima(i, 1, p)
                for p in PAR:
                    attended(i, 1, p)
                    dve.wait_ge(ao_ready, 4 * i + 3 + p)
                    v.tensor_tensor(x3[p][:], x2[p][:], ao[p][:], ALU.add).then_inc(x3_ready[p], 1)
                    dve.wait_ge(x3_ready[p], i + 1)
                    stats_of(i, p, x3)
                for p in PAR:
                    normalise(i, p, 3, x3)
                if isinstance(i, int):
                    dequantise()
                for p in PAR:
                    key = ("fd", p)
                    wait_full(dve, key, i)
                    dve.wait_ge(xb_ready[p], i + 1)
                    wait_at_least(dve, stored[p], 16 * i)
                    v.tensor_tensor(xo[p][:], xb[p][:], work_bank(key)[:, 0:D], ALU.add).then_inc(work_sem(key), 1)

            def dequantise():
                dve.wait_ge(ld_ffn, LD_FFN)
                for q, s in ((upq_sb, ups_sb), (dnq_sb, dns_sb)):
                    v.scalar_tensor_tensor(s[:], q[:], -7.5, s[:], ALU.add, ALU.mult).then_inc(deq_tmp, 1)
                dve.wait_ge(deq_tmp, 2)
                for w, s in ((upw, ups_sb), (dnw, dns_sb)):
                    v.tensor_tensor(w[:], w[:], s[:], ALU.add).then_inc(deq_ready, 1)

            iterations(dve, body)
            assert step["k"] == VSTEPS, step["k"]

        @block.tensor
        def _(pe):
            t_ = nc.tensor
            pe.wait_ge(ld_lora, 64)
            for b in range(4):
                t_.matmul(all_banks[b][:], upa_sb[:, (b // 2) * P:(b // 2 + 1) * P], upb_sb[:, (b % 2) * 512:(b % 2 + 1) * 512],
                          start=True, stop=True).then_inc(lora_mm, 1)
            for b in range(4):
                for c in range(2):
                    last = t_.matmul(all_banks[4 + b][:, c * D:(c + 1) * D], dna_sb[:, (2 * b + c) * P:(2 * b + c + 1) * P], dnb_sb[:],
                                     start=True, stop=True)
                last.then_inc(lora_mm, 1)
            pe.wait_ge(lora_copied, 8)
            pe.wait_ge(const_ready, N_CONST)
            pe.wait_ge(ld_kq, 32)

            def transpose_rows(i, key, src):
                wait_free(pe, key, i)
                for c in range(DC):
                    last = t_.transpose(work_bank(key)[:, c * P:(c + 1) * P], src[:, c * P:(c + 1) * P], idf[:])
                last.then_inc(w_full, 1)

            def transpose_heads(i, key, tiles):
                wait_free(pe, key, i)
                bank = work_bank(key)[:].bitcast(BF16)
                for k, tile in enumerate(tiles):
                    last = t_.transpose(bank[:, k * P:(k + 1) * P], tile, idb[:])
                last.then_inc(w_full, 1)

            def natural(i, layer, p):
                for t in range((NH1 if layer else NH0) // 4):
                    n = scores.index((layer, p, t))
                    wait_at_least(pe, max_ready, NS * i + n - 1)
                    bank = ps_nat[n % 2]
                    if layer:
                        u = t // 2
                        for jj in range(2):
                            j = 2 * (t % 2) + jj
                            last = t_.matmul(bank[:, jj * 2 * P:(jj + 1) * 2 * P], qt1[p][:, 4 * u + j, :], kz1[p][:, 2 * u:2 * u + 2, :],
                                             start=True, stop=True)
                    else:
                        t_.matmul(bank[:], idb[:], maskq[:], start=True, stop=False, skip_group_check=True)
                        for j in range(4):
                            h = 4 * t + j
                            last = t_.matmul(bank[:, j * P:(j + 1) * P], qt0[p][:, h, :], kt0[p][:, h, :], start=False, stop=True,
                                             skip_group_check=True)
                    last.then_inc(nat_full, 1)

            def transpose_maxima(i, layer, p):
                key = (f"mt{layer}", p)
                pe.wait_ge(mexp_ready[p], 2 * i + layer + 1)
                mexp = (mexp1 if layer else mexp0)[p]
                transpose_heads(i, key, [mexp[:, j, :] for j in range(G1)])

            def shifted(i, layer, p, t):
                n = scores.index((layer, p, t))
                wait_at_least(pe, exp_ready, NS * i + n - 1)
                bank = ps_tr[n % 2]
                if layer:
                    t_.matmul(bank[:], selg[:, t, :], mt[p][:], start=True, stop=False)
                    last = t_.matmul(bank[:], kz1[p][:, t, :], qt1[p][:, 4 * (t // 2):4 * (t // 2) + 4, :], start=False, stop=True)
                else:
                    t_.matmul(bank[:], idb[:], maskk[:], start=True, stop=False, skip_group_check=True)
                    t_.matmul(bank[:], selg[:, t, :], mt[p][:], start=False, stop=False, skip_group_check=True)
                    for j in range(4):
                        h = 4 * t + j
                        last = t_.matmul(bank[:, j * P:(j + 1) * P], kt0[p][:, h, :], qt0[p][:, h, :], start=False, stop=True,
                                         skip_group_check=True)
                last.then_inc(tr_full, 1)

            def weigh_values(i, layer, p, t):
                n = scores.index((layer, p, t))
                pe.wait_ge(exp_ready, NS * i + n + 1)
                if t == 0:
                    wait_at_least(pe, ao_ready, 4 * i + 2 * layer + p)
                w = (HD1 if layer else HD0) + 1
                for j in range(4):
                    h = 4 * t + j
                    value = va1[p][:, t, :] if layer else va0[p][:, h, :]
                    last = t_.matmul(ps_pv[:, h * w:(h + 1) * w], pt[n % NPT][:, j, :], value, start=True, stop=True)
                last.then_inc(pv_done, 1)

            def attention(i, layer):
                todo = []
                for p in PAR:
                    wait_read(pe, (f"mt{layer}", p), i)
                    for t in range((NH1 if layer else NH0) // 4):
                        shifted(i, layer, p, t)
                        todo.append((p, t))
                        if len(todo) > 2:
                            weigh_values(i, layer, *todo.pop(0))
                for p, t in todo:
                    weigh_values(i, layer, p, t)

            def body(i):
                for p in PAR:
                    key = ("ct", p)
                    pe.wait_ge(c_in[p], 16 * (i + 1))
                    wait_free(pe, key, i)
                    detach(pe)
                    t_.transpose(work_bank(key)[0:L, 0:P], cin[p][:], idf[:]).then_inc(w_full, 1)
                for p in PAR:
                    key = ("kv", p)
                    wait_read(pe, ("ct", p), i)
                    wait_free(pe, key, i)
                    t_.matmul(work_bank(key)[:], ct[p][:], wkv_sb[:], start=True, stop=True).then_inc(w_full, 1)
                for p in PAR:
                    pe.wait_ge(kexp1_ready[p], i + 1)
                    transpose_heads(i, ("kt1", p), [kexp1[p][:, 2 * u:2 * u + 2, :].rearrange("p g s -> p (g s)") for u in range(KV1 // 2)])
                    pe.wait_ge(kexp0_ready[p], i + 1)
                    for c in range(2):
                        transpose_heads(i, ("kt0", p, c), [kexp0[p][:, 8 * c + k, :] for k in range(8)])
                for p in PAR:
                    pe.wait_ge(xhat_ready[p], 4 * i + 1)
                    transpose_rows(i, ("xt0", p), xhat[p])
                for p in PAR:
                    key = ("q0", p)
                    wait_read(pe, ("xt0", p), i)
                    wait_free(pe, key, i)
                    for c in range(DC):
                        last = t_.matmul(work_bank(key)[:, 0:D], xht[p][:, c, :], wq_sb[:, c, :], start=c == 0, stop=c == DC - 1)
                    last.then_inc(w_full, 1)
                for p in PAR:
                    pe.wait_ge(qexp_ready[p], 2 * i + 1)
                    for c in range(2):
                        transpose_heads(i, ("qt0", p, c), [qexp0[p][:, 8 * c + k, :] for k in range(8)])
                for p in PAR:
                    wait_read(pe, ("kt0", p, 1), i)
                    wait_read(pe, ("qt0", p, 1), i)
                    natural(i, 0, p)
                for p in PAR:
                    transpose_maxima(i, 0, p)
                attention(i, 0)
                if isinstance(i, int):
                    pe.wait_ge(ld_out, 16)
                for p in PAR:
                    pe.wait_ge(ao_ready, 4 * i + p + 1)
                    transpose_rows(i, ("aot", p), ao[p])
                for p in PAR:
                    key = ("o0", p)
                    wait_read(pe, ("aot", p), i)
                    wait_free(pe, key, i)
                    for c in range(DC):
                        last = t_.matmul(work_bank(key)[:, 0:D], aot[p][:, c, :], wout_sb[:, c, :], start=c == 0, stop=c == DC - 1)
                    last.then_inc(w_full, 1)
                for p in PAR:
                    pe.wait_ge(xhat_ready[p], 4 * i + 2)
                    transpose_rows(i, ("xtm", p), xhat[p])
                if isinstance(i, int):
                    pe.wait_ge(ld_moe, 48)
                for p in PAR:
                    key = ("rt", p)
                    wait_read(pe, ("xtm", p), i)
                    wait_free(pe, key, i)
                    for c in range(DC):
                        last = t_.matmul(work_bank(key)[:, 0:E], xmt[:, c, p * P:(p + 1) * P], wr_sb[:, c, :], start=c == 0, stop=c == DC - 1)
                    last.then_inc(w_full, 1)

                def gate_up(t):
                    key = ("gu", t)
                    wait_free(pe, key, i)
                    for n, w in enumerate((wg_sb, wu_sb)):
                        for c in range(DC):
                            last = t_.matmul(work_bank(key)[:, n * 2 * P:(n + 1) * 2 * P], w[:, c, t * P:(t + 1) * P], xmt[:, c, :],
                                             start=c == 0, stop=c == DC - 1)
                    last.then_inc(w_full, 1)

                gate_up(0)
                gate_up(1)
                for p in PAR:
                    pe.wait_ge(wexp_ready[p], i + 1)
                    transpose_heads(i, ("wt", p), [wexp[p][:]])
                gate_up(2)
                wait_read(pe, ("wt", 0), i)
                wait_read(pe, ("wt", 1), i)
                for k in range(FT // 2):
                    key = ("wb", k)
                    wait_free(pe, key, i)
                    sel = sele[:].rearrange("p e f -> p (e f)")
                    for n in range(2):
                        t = 2 * k + n
                        last = t_.matmul(work_bank(key)[:, n * 2 * P:(n + 1) * 2 * P], sel[:, t * P:(t + 1) * P], wt[:], start=True, stop=True)
                    last.then_inc(w_full, 1)
                for t in range(3, FT):
                    gate_up(t)
                if isinstance(i, int):
                    pe.wait_ge(ld_down, 16)
                pe.wait_ge(hid_ready, FT * (i + 1))
                for p in PAR:
                    key = ("dn", p)
                    wait_free(pe, key, i)
                    for t in range(FT):
                        last = t_.matmul(work_bank(key)[:, 0:D], hid[:, t, p * P:(p + 1) * P], wd_sb[:, t, :], start=t == 0, stop=t == FT - 1)
                    last.then_inc(w_full, 1)
                for p in PAR:
                    pe.wait_ge(qexp_ready[p], 2 * i + 2)
                    for c in range(2):
                        transpose_heads(i, ("qt1", p, c), [qexp1[p][:, 2 * k:2 * k + 2, :].rearrange("p h s -> p (h s)") for k in range(8 * c, 8 * c + 8)])
                for p in PAR:
                    wait_read(pe, ("kt1", p), i)
                    wait_read(pe, ("qt1", p, 1), i)
                    natural(i, 1, p)
                for p in PAR:
                    transpose_maxima(i, 1, p)
                attention(i, 1)
                for p in PAR:
                    pe.wait_ge(xhat_ready[p], 4 * i + 4)
                    transpose_rows(i, ("xtf", p), xhat[p])
                for p in PAR:
                    wait_read(pe, ("xtf", p), i)
                if isinstance(i, int):
                    pe.wait_ge(deq_ready, 2)
                for k in range(HT // 2):
                    key = ("up", k)
                    wait_free(pe, key, i)
                    for n in range(2):
                        t = 2 * k + n
                        for c in range(DC):
                            last = t_.matmul(work_bank(key)[:, n * 2 * P:(n + 1) * 2 * P], upw[:, c, t * P:(t + 1) * P], xft[:, c, :],
                                             start=c == 0, stop=c == DC - 1)
                    last.then_inc(w_full, 1)
                for k in range(HT // 2):
                    wait_read(pe, ("up", k), i)
                for p in PAR:
                    key = ("fd", p)
                    wait_free(pe, key, i)
                    for t in range(HT):
                        last = t_.matmul(work_bank(key)[:, 0:D], hft[:, t, p * P:(p + 1) * P], dnw[:, t, :], start=t == 0, stop=t == HT - 1)
                    last.then_inc(w_full, 1)

            iterations(pe, body)

    return nc


_INS = ["x", "ctx", "wq", "wkv", "wout", "wr", "wg", "wu", "wd", "upq", "ups", "bup", "upa", "upb", "dnq", "dns", "bdn", "dna", "dnb"]


def kernel(x, ctx_512, L0_xattn_Wq, L0_xattn_Wkv_expand, L0_xattn_Wout, L0_ffn_w_gate_router, L0_ffn_w_gate_proj,
           L0_ffn_w_up_proj, L0_ffn_w_down_proj, L1_ffn_w_up_q, L1_ffn_w_up_scale, L1_ffn_b_up, L1_ffn_w_up_lora_a,
           L1_ffn_w_up_lora_b, L1_ffn_w_down_q, L1_ffn_w_down_scale, L1_ffn_b_down, L1_ffn_w_down_lora_a, L1_ffn_w_down_lora_b):
    import numpy as np
    import concourse.bacc as bacc
    from concourse.bass_utils import run_bass_kernel_spmd

    laid = {
        "x": np.asarray(x), "ctx": np.asarray(ctx_512),
        "wq": np.asarray(L0_xattn_Wq).T, "wkv": np.asarray(L0_xattn_Wkv_expand).T, "wout": np.asarray(L0_xattn_Wout).T,
        "wr": np.asarray(L0_ffn_w_gate_router).T,
        "wg": np.asarray(L0_ffn_w_gate_proj).reshape(E * F, D).T, "wu": np.asarray(L0_ffn_w_up_proj).reshape(E * F, D).T,
        "wd": np.asarray(L0_ffn_w_down_proj).transpose(0, 2, 1).reshape(E * F, D),
        "upq": np.asarray(L1_ffn_w_up_q).T, "ups": np.asarray(L1_ffn_w_up_scale).T,
        "bup": np.asarray(L1_ffn_b_up).reshape(HT, P).T,
        "upa": np.asarray(L1_ffn_w_up_lora_a).T, "upb": np.asarray(L1_ffn_w_up_lora_b),
        "dnq": np.asarray(L1_ffn_w_down_q).T, "dns": np.asarray(L1_ffn_w_down_scale).T,
        "bdn": np.asarray(L1_ffn_b_down).reshape(1, D),
        "dna": np.asarray(L1_ffn_w_down_lora_a).T, "dnb": np.asarray(L1_ffn_w_down_lora_b),
    }
    nc = bacc.Bacc("TRN2", target_bir_lowering=False, num_devices=1)
    arrays, args = {}, []
    for name in _INS:
        a = np.ascontiguousarray(laid[name])
        arrays[f"in_{name}_dram"] = a
        args.append(nc.dram_tensor(f"in_{name}_dram", a.shape, mybir.dt.from_np(a.dtype), kind="ExternalInput").ap())
    out = nc.dram_tensor("out_dram", laid["x"].shape, F32, kind="ExternalOutput").ap()
    build(nc, *args, out)
    r = run_bass_kernel_spmd(nc, [arrays], core_ids=[0])
    return r.results[0]["out_dram"]
```

```python
from contextlib import ExitStack

import concourse.bass as bass
from concourse import mybir

F32 = mybir.dt.float32
BF16 = mybir.dt.bfloat16
I32 = mybir.dt.int32
U32 = mybir.dt.uint32
ALU = mybir.AluOpType
ACT = mybir.ActivationFunctionType
AX_X = mybir.AxisListType.X

P = 128
D = 256
DC = D // P
L = 64
NH0, HD0 = 16, 16
NH1, KV1, HD1 = 32, 8, 8
G1 = NH1 // KV1
E, F = 8, 96
FT = E * F // P
H = 1024
HT = H // P
R = 16
BLOCK = 64
W0 = NH0 * (HD0 + 1)
W1 = NH1 * (HD1 + 1)
EPS = 1e-5
MASKED = -1e30
TERMS = 6

Q_PARTS = {"h": (0, 3), "m": (3, 5), "l": (5, 6)}


LAG = {"P": 0,
       "A": 0,
       "M": 1,
       "K": 1,
       "B": 2,
       "F": 2}
DEPTH = max(LAG.values())


class Uses:

    def __init__(self, order, banks, rows):
        self.order, self.banks, self.rows = order, banks, rows

    def active(self, key, t):
        return 0 <= t - LAG[key[0]] < self.rows

    def bank(self, key):
        return self.order.index(key) % self.banks

    def before(self, key, t, bank=None):
        mine = [k for k in self.order if bank is None or self.bank(k) == bank]
        if not isinstance(t, int):
            return self.before(key, DEPTH, bank) + (t - DEPTH) * len(mine)
        n = sum(self.active(k, u) for u in range(t) for k in mine)
        return n + sum(self.active(k, t) for k in mine if self.order.index(k) < self.order.index(key))

    def at_start(self, t, bank):
        mine = [k for k in self.order if self.bank(k) == bank]
        if not isinstance(t, int):
            return self.at_start(DEPTH, bank) + (t - DEPTH) * len(mine)
        return sum(self.active(k, u) for u in range(t) for k in mine)


def build(nc, x, ctx, wq, wkv, wout, wr, wg, wu, wd, upq, ups, bup, upa, upb, dnq, dns, bdn, dna, dnb, out):
    ROWS = x.shape[0]
    N0, N1 = NH0 // 4, NH1 // 4
    NPT = 4

    work = Uses([("M", "xt"), ("B", "kt"), ("M", "rt"), ("P", "ct"), ("M", "gu", 0), ("P", "kv"), ("P", "xt"), ("M", "gu", 1),
                 ("P", "q"), ("P", "kt", 0), ("P", "kt", 1), ("M", "gu", 2), ("P", "qt", 0), ("P", "qt", 1), ("M", "wt"),
                 ("M", "wb", 0), ("M", "wb", 1), ("M", "dn"), ("F", "xt"), ("F", "up", 0), ("F", "up", 1), ("F", "fd")], 2, ROWS)
    near = Uses([("B", "qt", 0), ("B", "qt", 1)] + [("B", "nat", k) for k in range(N1)] + [("B", "mt")]
                + [("A", "nat", k) for k in range(N0)] + [("A", "mt"), ("A", "at"), ("A", "out")], 2, ROWS)
    far = Uses([("B", "s", k) for k in range(N1)] + [("A", "s", k) for k in range(N0)], 2, ROWS)

    with ExitStack() as stack:
        def sb(name, shape, dt=F32):
            return stack.enter_context(nc.sbuf_tensor(name, shape, dt))

        def psum(name, shape, dt=F32):
            return stack.enter_context(nc.psum_tensor(name, shape, dt))

        def sem(name):
            return stack.enter_context(nc.semaphore(name))

        def sems(name, n=2):
            return [sem(f"{name}{k}") for k in range(n)]

        wq_sb = sb("wq_sb", [P, DC, D])
        wkv_sb = sb("wkv_sb", [L, 2 * D])
        wout_sb = sb("wout_sb", [P, DC, D])
        wr_sb = sb("wr_sb", [P, DC, E])
        wg_sb = sb("wg_sb", [P, DC, E * F])
        wu_sb = sb("wu_sb", [P, DC, E * F])
        wd_sb = sb("wd_sb", [P, FT, D])
        upq_sb = sb("upq_sb", [P, DC, H], I32)
        dnq_sb = sb("dnq_sb", [P, HT, D], I32)
        ups_sb = sb("ups_sb", [P, DC, H])
        dns_sb = sb("dns_sb", [P, HT, D])
        upw = sb("upw", [P, DC, H])
        dnw = sb("dnw", [P, HT, D])
        bup_sb = sb("bup_sb", [P, HT])
        bdn_sb = sb("bdn_sb", [P, D])
        upa_sb = sb("upa_sb", [R, D])
        upb_sb = sb("upb_sb", [R, H])
        dna_sb = sb("dna_sb", [R, H])
        dnb_sb = sb("dnb_sb", [R, D])
        idf = sb("idf", [P, P])
        idb = sb("idb", [P, P], BF16)
        maskq = sb("maskq", [P, 4, P], BF16)
        maskk = sb("maskk", [P, 4, P], BF16)
        selg = sb("selg", [P, KV1, P], BF16)
        sele = sb("sele", [P, E, F], BF16)
        mhalf = sb("mhalf", [P, 1])
        expert = sb("expert", [P, E])
        cin = sb("cin", [P, L])
        xin = sb("xin", [P, D])
        ct = sb("ct", [L, P])
        kres = sb("kres", [P, D])
        kexp0 = sb("kexp0", [P, NH0, P], BF16)
        qres0 = sb("qres0", [P, D])
        qexp0 = sb("qexp0", [P, NH0, P], BF16)
        xht0 = sb("xht0", [P, DC, P])
        kt0 = sb("kt0", [P, NH0, P], BF16)
        qt0 = sb("qt0", [P, NH0, P], BF16)
        va0 = sb("va0", [P, NH0, HD0 + 1])
        norms = ("P", "A", "M", "B")
        stats = {s: sb(f"stats{s}", [P, 6]) for s in norms}
        mv = {s: sb(f"mv{s}", [P, 2]) for s in norms}
        var_eps = {s: sb(f"var_eps{s}", [P, 1]) for s in norms}
        rstd = {s: sb(f"rstd{s}", [P, 1]) for s in norms}
        xhat = {s: sb(f"xhat{s}", [P, D]) for s in norms}
        nmax = {s: sb(f"nmax{s}", [P, G1, KV1]) for s in "AB"}
        mexp = {s: sb(f"mexp{s}", [P, G1, P], BF16) for s in "AB"}
        mt = {s: sb(f"mt{s}", [P, G1 * P], BF16) for s in "AB"}
        pt = [sb(f"pt{k}", [P, 4, P]) for k in range(NPT)]
        rden = {s: sb(f"rden{s}", [P, NH1]) for s in "AB"}
        ao = {s: sb(f"ao{s}", [P, D]) for s in "AB"}
        aot = sb("aot", [P, DC, P])
        xres = sb("xres", [P, D])
        x1 = sb("x1", [P, D])
        xht1 = sb("xht1", [P, DC, P])
        score = sb("score", [P, E])
        top8 = sb("top8", [P, 8])
        idx8 = sb("idx8", [P, 8], U32)
        idxf = sb("idxf", [P, 2])
        gap = sb("gap", [P, 1])
        egap = sb("egap", [P, 1])
        den2 = sb("den2", [P, 1])
        p12 = sb("p12", [P, 2])
        w1st = sb("w1st", [P, E])
        w2nd = sb("w2nd", [P, E])
        wtok = sb("wtok", [P, E])
        wres = sb("wres", [P, E])
        wexp = sb("wexp", [P, P], BF16)
        wt = sb("wt", [P, P], BF16)
        wb = sb("wb", [P, FT, P])
        th = sb("th", [P, FT, P])
        sg = sb("sg", [P, FT, P])
        su = sb("su", [P, FT, P])
        hid = sb("hid", [P, FT, P])
        x2 = sb("x2", [P, D])
        qres1 = sb("qres1", [P, D])
        qexp1 = sb("qexp1", [P, NH1, L], BF16)
        cinb = sb("cinb", [P, L])
        kres1 = sb("kres1", [P, L])
        kexp1 = sb("kexp1", [P, KV1, L], BF16)
        kz1 = sb("kz1", [P, KV1, P], BF16)
        va1 = sb("va1", [P, KV1, HD1 + 1])
        qt1 = sb("qt1", [P, NH1 // 2, P], BF16)
        x3 = sb("x3", [P, D])
        xb = sb("xb", [P, D])
        xht3 = sb("xht3", [P, DC, P])
        hft = sb("hft", [P, HT, P])
        xo = sb("xo", [P, D])

        ps_work = [psum(f"ps_work{k}", [P, 512]) for k in range(2)]
        ps_near = [psum(f"ps_near{k}", [P, 512]) for k in range(2)]
        ps_far = [psum(f"ps_far{k}", [P, 512]) for k in range(2)]
        ps_pv = {s: psum(f"ps_pv{s}", [P, 512]) for s in "AB"}
        lora_banks = ps_near + ps_far + [ps_pv["A"], ps_pv["B"]] + ps_near

        c_in, x_in, xres_in, cinb_in = sem("c_in"), sem("x_in"), sem("xres_in"), sem("cinb_in")
        ld_kv, ld_q, ld_out, ld_moe, ld_down, ld_lora, ld_ffn = (sem(f"ld_{n}") for n in
                                                                 ("kv", "q", "out", "moe", "down", "lora", "ffn"))
        stored = sem("stored")
        pool_set, ident_ready, const_ready, zeroed_ready = sem("pool_set"), sem("ident_ready"), sem("const_ready"), sem("zeroed_ready")
        lora_mm, lora_copied = sem("lora_mm"), sem("lora_copied")
        deq_tmp, deq_ready = sem("deq_tmp"), sem("deq_ready")
        work.full, work.read, work.ps = sem("work_full"), sems("work_read"), ps_work
        near.full, near.read, near.ps = sem("near_full"), sems("near_read"), ps_near
        far.full, exp_ready, pv_done = sem("far_full"), sem("exp_ready"), sem("pv_done")
        ln_var, ln_pool, ln_rstd, xhat_ready = ({s: sem(f"{n}{s}") for s in norms} for n in
                                                ("ln_var", "ln_pool", "ln_rstd", "xhat_ready"))
        v0_ready, kh0_ready, km0_ready, kexp0_ready = sem("v0_ready"), sem("kh0_ready"), sem("km0_ready"), sem("kexp0_ready")
        v1_ready, kh1_ready, kres1_ready, km1_ready, kexp1_ready = (sem(n) for n in (
            "v1_ready", "kh1_ready", "kres1_ready", "km1_ready", "kexp1_ready"))
        qh0_ready, qm0_ready, qexp0_ready = sem("qh0_ready"), sem("qm0_ready"), sem("qexp0_ready")
        qh1_ready, qres1_ready, qm1_ready, qexp1_ready = sem("qh1_ready"), sem("qres1_ready"), sem("qm1_ready"), sem("qexp1_ready")
        mhigh_ready, mexp_ready, ao_ready = ({s: sem(f"{n}{s}") for s in "AB"} for n in ("mhigh_ready", "mexp_ready", "ao_ready"))
        x3_ready, xb_ready = sem("x3_ready"), sem("xb_ready")
        gap_ready, egap_ready, wexp_ready = sem("gap_ready"), sem("egap_ready"), sem("wexp_ready")
        th_ready, sg_ready, hid_ready = sem("th_ready"), sem("sg_ready"), sem("hid_ready")
        vstep = {s: sem(f"vstep{s}") for s in LAG}

        block = stack.enter_context(nc.Block())
        LD_FFN = 16 * 10
        VSTEPS = {"P": 1, "A": 2, "M": 12, "K": 0, "B": 2, "F": 0}
        N_CONST, N_ZEROED = 7, 10

        def wait_at_least(eng, s, count):
            if not isinstance(count, int) or count > 0:
                eng.wait_ge(s, count)

        def detach(eng):
            eng.nop(nofuse=True)

        def bank(ring, key):
            return ring.ps[ring.bank(key)]

        def read_sem(ring, key):
            return ring.read[ring.bank(key)]

        def wait_free(eng, ring, key, t):
            wait_at_least(eng, read_sem(ring, key), ring.before(key, t, ring.bank(key)))

        def wait_full(eng, ring, key, t):
            eng.wait_ge(ring.full, ring.before(key, t) + 1)

        def wait_read(eng, ring, key, t):
            eng.wait_ge(read_sem(ring, key), ring.before(key, t, ring.bank(key)) + 1)

        def row_of(stage, t):
            return t - LAG[stage]

        def has_row(stage, t):
            return not isinstance(t, int) or 0 <= row_of(stage, t) < ROWS

        def pipeline(eng, body):
            for t in range(DEPTH):
                body(t)
            with eng.Fori(DEPTH, ROWS) as t:
                body(t)
            for t in range(ROWS, ROWS + DEPTH):
                body(t)

        def heads(ap, hd):
            return ap.rearrange("p (h d) -> p h d", d=hd)

        def slots(exp, hd):
            return exp[:, :, 0:TERMS * hd].rearrange("p h (s d) -> p h s d", d=hd)

        def repeated(ap, n, hd):
            return ap.rearrange("p (h s d) -> p h s d", s=1, d=hd).broadcast_to([P, ap.shape[1] // hd, n, hd])

        def dram_row(ap, r):
            return ap[bass.ds(r, 1), :, :].rearrange("a t c -> t (a c)")

        @block.sync
        def _(sp):
            def weights():
                sp.dma_start(wout_sb[:], wout.rearrange("(c p) n -> p c n", p=P)).then_inc(ld_out, 16)
                sp.dma_start(wr_sb[:], wr.rearrange("(c p) n -> p c n", p=P)).then_inc(ld_moe, 16)
                sp.dma_start(wg_sb[:], wg.rearrange("(c p) n -> p c n", p=P)).then_inc(ld_moe, 16)
                sp.dma_start(wu_sb[:], wu.rearrange("(c p) n -> p c n", p=P)).then_inc(ld_moe, 16)
                sp.dma_start(wd_sb[:], wd.rearrange("(c p) n -> p c n", p=P)).then_inc(ld_down, 16)
                for c in range(DC):
                    for half in range(2):
                        sp.dma_start(ups_sb[half * BLOCK:(half + 1) * BLOCK, c, :],
                                     ups[2 * c + half:2 * c + half + 1, :].broadcast_to([BLOCK, H])).then_inc(ld_ffn, 16)
                for half in range(2):
                    sp.dma_start(dns_sb[half * BLOCK:(half + 1) * BLOCK, :, :],
                                 dns.rearrange("(c a) n -> a c n", a=2)[half:half + 1, :, :].broadcast_to([BLOCK, HT, D])).then_inc(ld_ffn, 16)
                sp.dma_start(upq_sb[:], upq.rearrange("(c p) n -> p c n", p=P)).then_inc(ld_ffn, 16)
                sp.dma_start(dnq_sb[:], dnq.rearrange("(c p) n -> p c n", p=P)).then_inc(ld_ffn, 16)
                sp.dma_start(bup_sb[:], bup).then_inc(ld_ffn, 16)
                sp.dma_start(bdn_sb[:], bdn.broadcast_to([P, D])).then_inc(ld_ffn, 16)

            def body(t):
                if has_row("P", t):
                    r = row_of("P", t)
                    if not isinstance(t, int) or t > 0:
                        sp.wait_ge(v0_ready, r)
                        sp.wait_ge(xhat_ready["P"], r)
                    sp.dma_start(cin[:], dram_row(ctx, r)).then_inc(c_in, 16)
                    sp.dma_start(xin[:], dram_row(x, r)).then_inc(x_in, 16)
                if isinstance(t, int) and t == 0:
                    sp.dma_start(wkv_sb[:], wkv).then_inc(ld_kv, 16)
                    sp.dma_start(wq_sb[:], wq.rearrange("(c p) n -> p c n", p=P)).then_inc(ld_q, 16)
                if has_row("F", t - 1):
                    wait_read(sp, work, ("F", "fd"), t - 1)
                    sp.dma_start(dram_row(out, row_of("F", t - 1)), xo[:]).then_inc(stored, 16)
                if has_row("A", t):
                    r = row_of("A", t)
                    if not isinstance(t, int) or r > 0:
                        sp.wait_ge(ln_var["A"], r)
                    sp.dma_start(xres[:], dram_row(x, r)).then_inc(xres_in, 16)
                if isinstance(t, int) and t == 0:
                    weights()
                if has_row("K", t):
                    r = row_of("K", t)
                    if not isinstance(t, int) or r > 0:
                        sp.wait_ge(kexp1_ready, r)
                        sp.wait_ge(v1_ready, r)
                    sp.dma_start(cinb[:], dram_row(ctx, r)).then_inc(cinb_in, 16)

            for t in range(DEPTH + 1):
                body(t)
            with sp.Fori(DEPTH + 1, ROWS) as t:
                body(t)
            for t in range(ROWS, ROWS + DEPTH + 1):
                body(t)
            sp.wait_ge(stored, 16 * ROWS)

        @block.gpsimd
        def _(pool):
            g = nc.gpsimd
            zeroed = [idf, idb, maskq, maskk, selg, sele]
            for n, t in enumerate(zeroed):
                g.memset(t[:], 0.0).then_inc(pool_set, 1)

            def fill(t, value, pattern, base, cm, op=ALU.not_equal, ready=const_ready):
                g.affine_select(out=t, in_=t, compare_op=op, fill=value, base=base, pattern=pattern,
                                channel_multiplier=cm).then_inc(ready, 1)

            pool.wait_ge(pool_set, len(zeroed))
            fill(idf[:], 1.0, [[-1, P]], 0, 1, ready=ident_ready)
            fill(idb[:], 1.0, [[-1, P]], 0, 1, ready=ident_ready)
            g.memset(mhalf[:], -0.5).then_inc(pool_set, 1)
            fill(maskq[:], MASKED, [[0, 4], [-1, P]], 0, 1, ALU.is_ge)
            fill(maskk[:], MASKED, [[0, 4], [1, P]], 0, -1, ALU.is_ge)
            fill(selg[:], 1.0, [[-1, KV1], [0, P]], 0, 1)
            fill(sele[:], 0.5, [[-1, E], [0, F]], 0, 1)
            pool.wait_ge(const_ready, 4)
            fill(selg[:], 1.0, [[-1, KV1], [0, P]], -KV1, 1)
            fill(sele[:], 0.5, [[-1, E], [0, F]], -E, 1)
            pool.wait_ge(const_ready, 6)
            fill(sele[:], 0.5, [[-1, E], [0, F]], -2 * E, 1)
            pool.wait_ge(pool_set, len(zeroed) + 1)
            pool.wait_ge(zeroed_ready, N_ZEROED)

            def layernorm_rstd(s, t):
                if not has_row(s, t):
                    return
                r = row_of(s, t)
                pool.wait_ge(ln_var[s], r + 1)
                detach(pool)
                g.tensor_scalar(var_eps[s][:], mv[s][:, 1:2], EPS, None, ALU.add).then_inc(ln_pool[s], 1)
                pool.wait_ge(ln_pool[s], r + 1)
                g.tensor_tensor(rstd[s][:], var_eps[s][:], mhalf[:], ALU.pow).then_inc(ln_rstd[s], 1)

            def key_parts(t):
                if not has_row("K", t):
                    return
                r = row_of("K", t)
                pool.wait_ge(kh1_ready, r + 1)
                k1 = slots(kexp1, HD1)
                res = heads(kres1[:], HD1)
                g.tensor_tensor(res, heads(cinb[:], HD1), k1[:, :, 1, :], ALU.subtract).then_inc(kres1_ready, 1)
                pool.wait_ge(kres1_ready, r + 1)
                detach(pool)
                g.tensor_copy(k1[:, :, 2:5:2, :], repeated(kres1[:], 2, HD1)).then_inc(km1_ready, 1)
                pool.wait_ge(km1_ready, r + 1)
                g.tensor_tensor(k1[:, :, 0, :], res, k1[:, :, 2, :], ALU.subtract).then_inc(kexp1_ready, 1)

            def values(t):
                if not has_row("K", t):
                    return
                r = row_of("K", t)
                pool.wait_ge(cinb_in, 16 * (r + 1))
                wait_at_least(pool, ao_ready["B"], r)
                detach(pool)
                g.tensor_copy(va1[:, :, 0:HD1], heads(cinb[:], HD1)).then_inc(v1_ready, 1)

            def hidden_weighed(t, k):
                if not has_row("M", t):
                    return
                wait_read(pool, work, ("M", "gu", k), t)
                wait_read(pool, work, ("M", "wb", k // 2), t)
                g.tensor_tensor(hid[:, 2 * k:2 * k + 2, :], su[:, 2 * k:2 * k + 2, :], wb[:, 2 * k:2 * k + 2, :], ALU.mult).then_inc(hid_ready, 1)

            def body(t):
                layernorm_rstd("P", t)
                key_parts(t)
                for k in range(FT // 2):
                    hidden_weighed(t, k)
                layernorm_rstd("B", t)
                if has_row("B", t):
                    if isinstance(t, int):
                        pool.wait_ge(ld_ffn, LD_FFN)
                    g.tensor_tensor(xb[:], x3[:], bdn_sb[:], ALU.add).then_inc(xb_ready, 1)
                values(t)
                layernorm_rstd("M", t)
                layernorm_rstd("A", t)

            pipeline(pool, body)

        @block.scalar
        def _(act):
            a = nc.scalar
            act.dma_start(upa_sb[:], upa).then_inc(ld_lora, 16)
            act.dma_start(upb_sb[:], upb).then_inc(ld_lora, 16)
            act.dma_start(dna_sb[:], dna).then_inc(ld_lora, 16)
            act.dma_start(dnb_sb[:], dnb).then_inc(ld_lora, 16)

            def copy_lora():
                for b in range(4):
                    act.wait_ge(lora_mm, b + 1)
                    a.activation(upw[:, b // 2, (b % 2) * 512:(b % 2 + 1) * 512], lora_banks[b][:], ACT.Copy).then_inc(lora_copied, 1)
                for b in range(4):
                    act.wait_ge(lora_mm, 5 + b)
                    a.activation(dnw[:, 2 * b:2 * b + 2, :], heads(lora_banks[4 + b][:], D), ACT.Copy).then_inc(lora_copied, 1)

            def exps(s, t, k):
                if not has_row(s, t):
                    return
                key = (s, "s", k)
                n = far.before(key, t)
                act.wait_ge(far.full, n + 1)
                wait_at_least(act, pv_done, n - NPT + 1)
                a.activation(pt[far.order.index(key) % NPT][:], heads(ps_far[far.bank(key)][:], P), ACT.Exp,
                             scale=float(HD0 if s == "A" else HD1) ** -0.5).then_inc(exp_ready, 1)

            def copy_tiles(ring, key, dst, t):
                if has_row(key[0], t):
                    wait_full(act, ring, key, t)
                    a.activation(dst, heads(bank(ring, key)[:].bitcast(BF16), P), ACT.Copy).then_inc(read_sem(ring, key), 1)

            def transposed(ring, key, dst, t, n=DC):
                if has_row(key[0], t):
                    wait_full(act, ring, key, t)
                    a.activation(dst, heads(bank(ring, key)[:, 0:n * P], P), ACT.Copy).then_inc(read_sem(ring, key), 1)

            def keys_k(t):
                if has_row("K", t):
                    act.wait_ge(cinb_in, 16 * (row_of("K", t) + 1))
                    if has_row("B", t):
                        wait_full(act, work, ("B", "kt"), t)
                    a.activation(slots(kexp1, HD1)[:, :, 1:6:2, :], repeated(cinb[:], 3, HD1), ACT.Copy).then_inc(kh1_ready, 1)

            def keys_p(t):
                if has_row("P", t):
                    key = ("P", "kv")
                    wait_full(act, work, key, t)
                    kv = bank(work, key)
                    a.activation(slots(kexp0, HD0)[:, :, 1:6:2, :], repeated(kv[:, 0:D], 3, HD0), ACT.Copy).then_inc(kh0_ready, 1)
                    wait_at_least(act, ao_ready["A"], row_of("P", t))
                    a.activation(va0[:, :, 0:HD0], heads(kv[:, D:2 * D], HD0), ACT.Copy).then_inc(v0_ready, 1)

            def keys_p_middle(t):
                if has_row("P", t):
                    wait_read(act, work, ("P", "kv"), t)
                    a.activation(slots(kexp0, HD0)[:, :, 2:5:2, :], repeated(kres[:], 2, HD0), ACT.Copy).then_inc(km0_ready, 1)

            def queries_p(t):
                if has_row("P", t):
                    wait_full(act, work, ("P", "q"), t)
                    a.activation(slots(qexp0, HD0)[:, :, 0:3, :], repeated(bank(work, ("P", "q"))[:, 0:D], 3, HD0), ACT.Copy).then_inc(qh0_ready, 1)

            def queries_p_middle(t):
                if has_row("P", t):
                    wait_read(act, work, ("P", "q"), t)
                    a.activation(slots(qexp0, HD0)[:, :, 3:5, :], repeated(qres0[:], 2, HD0), ACT.Copy).then_inc(qm0_ready, 1)

            def queries_m(t):
                if has_row("M", t):
                    act.wait_ge(xhat_ready["M"], row_of("M", t) + 1)
                    a.activation(slots(qexp1, HD1)[:, :, 0:3, :], repeated(xhat["M"][:], 3, HD1), ACT.Copy).then_inc(qh1_ready, 1)

            def queries_m_middle(t):
                if has_row("M", t):
                    act.wait_ge(qres1_ready, row_of("M", t) + 1)
                    a.activation(slots(qexp1, HD1)[:, :, 3:5, :], repeated(qres1[:], 2, HD1), ACT.Copy).then_inc(qm1_ready, 1)

            def tanh(t, k):
                if has_row("M", t):
                    wait_full(act, work, ("M", "gu", k), t)
                    a.activation(th[:, 2 * k:2 * k + 2, :], heads(bank(work, ("M", "gu", k))[:, 0:2 * P], P), ACT.Tanh, scale=0.5).then_inc(th_ready, 1)

            def softmax_of_two(t):
                if has_row("M", t):
                    act.wait_ge(gap_ready, row_of("M", t) + 1)
                    a.activation(egap[:], gap[:], ACT.Exp).then_inc(egap_ready, 1)

            def relu(t, k):
                if has_row("F", t):
                    if isinstance(t, int):
                        act.wait_ge(ld_ffn, LD_FFN)
                    key = ("F", "up", k)
                    wait_full(act, work, key, t)
                    for n in range(4):
                        h = 4 * k + n
                        last = a.activation(hft[:, h, :], bank(work, key)[:, n * P:(n + 1) * P], ACT.Relu, bias=bup_sb[:, h:h + 1])
                    last.then_inc(read_sem(work, key), 1)

            def spread_weights(t, k):
                if has_row("M", t):
                    key = ("M", "wb", k)
                    n = 4 if k == 0 else FT - 4
                    wait_full(act, work, key, t)
                    a.activation(wb[:, 4 * k:4 * k + n, :], heads(bank(work, key)[:, 0:n * P], P), ACT.Copy).then_inc(read_sem(work, key), 1)

            def body(t):
                transposed(work, ("M", "xt"), xht1[:], t)
                copy_tiles(near, ("B", "qt", 1), qt1[:, 8:16, :], t)
                softmax_of_two(t)
                keys_k(t)
                tanh(t, 0)
                keys_p(t)
                transposed(work, ("P", "xt"), xht0[:], t)
                keys_p_middle(t)
                tanh(t, 1)
                queries_p(t)
                queries_p_middle(t)
                copy_tiles(work, ("P", "kt", 1), kt0[:, 8:16, :], t)
                tanh(t, 2)
                exps("B", t, 0)
                exps("B", t, 1)
                copy_tiles(work, ("P", "qt", 1), qt0[:, 8:16, :], t)
                for k in range(2, 5):
                    exps("B", t, k)
                spread_weights(t, 0)
                exps("B", t, 5)
                spread_weights(t, 1)
                exps("B", t, 6)
                exps("B", t, 7)
                exps("A", t, 0)
                exps("A", t, 1)
                exps("A", t, 2)
                transposed(work, ("F", "xt"), xht3[:], t)
                exps("A", t, 3)
                queries_m(t)
                relu(t, 0)
                queries_m_middle(t)
                transposed(near, ("A", "at"), aot[:], t)
                relu(t, 1)

            copy_lora()
            act.wait_ge(zeroed_ready, N_ZEROED)
            pipeline(act, body)

        @block.vector
        def _(dve):
            v = nc.vector
            now, steps = {}, {}

            def done(s, ins):
                steps[s] += 1
                ins.then_inc(vstep[s], 1)
                dve.wait_ge(vstep[s], VSTEPS[s] * row_of(s, now["t"]) + steps[s])

            def stats_of(s, src):
                done(s, v.bn_stats(stats[s][:], src[:]))
                detach(dve)
                v.bn_aggr(mv[s][:], stats[s][:]).then_inc(ln_var[s], 1)

            def normalise(s, t, src):
                dve.wait_ge(ln_rstd[s], row_of(s, t) + 1)
                v.tensor_scalar(xhat[s][:], src[:], mv[s][:, 0:1], rstd[s][:], ALU.subtract, ALU.mult).then_inc(xhat_ready[s], 1)

            def copy_transposes(ring, key, dst, t):
                if has_row(key[0], t):
                    wait_full(dve, ring, key, t)
                    v.tensor_copy(dst, heads(bank(ring, key)[:].bitcast(BF16), P)).then_inc(read_sem(ring, key), 1)

            def maximum(s, t, k):
                if not has_row(s, t):
                    return
                key = (s, "nat", k)
                wait_full(dve, near, key, t)
                src = bank(near, key)[:]
                if s == "B":
                    u, j = k // 2, 2 * (k % 2)
                    src = src.rearrange("p (j g k) -> p j g k", j=2, g=2)
                    dst = nmax[s][:, j:j + 2, 2 * u:2 * u + 2]
                else:
                    src = src.rearrange("p (j k) -> p j k", j=4)
                    dst = nmax[s][:, :, k]
                v.tensor_reduce(dst, src, AX_X, ALU.max, negate=True).then_inc(read_sem(near, key), 1)

            def maximum_parts(s, t):
                if not has_row(s, t):
                    return
                groups = KV1 if s == "B" else N0
                for k in range(2):
                    wait_read(dve, near, (s, "nat", (N1 if s == "B" else N0) - 1 - k), t)
                m = mexp[s]
                r = row_of(s, t)
                v.tensor_copy(m[:, :, 0:groups], nmax[s][:, :, 0:groups]).then_inc(mhigh_ready[s], 1)
                dve.wait_ge(mhigh_ready[s], r + 1)
                v.tensor_tensor(m[:, :, KV1:KV1 + groups], nmax[s][:, :, 0:groups], m[:, :, 0:groups],
                                ALU.subtract).then_inc(mexp_ready[s], 1)

            def copy_maxima(s, t):
                if has_row(s, t):
                    key = (s, "mt")
                    wait_full(dve, near, key, t)
                    v.tensor_copy(mt[s][:], bank(near, key)[:, 0:2 * P].bitcast(BF16)).then_inc(read_sem(near, key), 1)

            def attended(s, t):
                nh, hd = (NH1, HD1) if s == "B" else (NH0, HD0)
                dve.wait_ge(pv_done, far.before((s, "s", nh // 4 - 1), t) + 1)
                o = ps_pv[s][:, 0:nh * (hd + 1)].rearrange("p (h d) -> p h d", d=hd + 1)
                r = rden[s][:, 0:nh].rearrange("p (h d) -> p h d", d=1)
                done(s, v.reciprocal(r, o[:, :, hd:hd + 1]))
                v.tensor_tensor(heads(ao[s][:], hd), o[:, :, 0:hd], r.broadcast_to([P, nh, hd]), ALU.mult).then_inc(ao_ready[s], 1)

            def norm_p(t):
                if has_row("P", t):
                    dve.wait_ge(x_in, 16 * (row_of("P", t) + 1))
                    stats_of("P", xin)

            def router(t):
                if not has_row("M", t):
                    return
                key = ("M", "rt")
                wait_full(dve, work, key, t)
                v.tensor_copy(score[:], bank(work, key)[:, 0:E]).then_inc(read_sem(work, key), 1)
                wait_read(dve, work, key, t)
                detach(dve)
                done("M", v.max(top8[:], score[:]))
                v.tensor_tensor(gap[:], top8[:, 1:2], top8[:, 0:1], ALU.subtract).then_inc(gap_ready, 1)
                detach(dve)
                done("M", v.max_index(idx8[:], top8[:], score[:]))
                done("M", v.tensor_copy(idxf[:], idx8[:, 0:2]))

            def router_weights(t):
                if not has_row("M", t):
                    return
                dve.wait_ge(egap_ready, row_of("M", t) + 1)
                done("M", v.tensor_scalar(den2[:], egap[:], 1.0, None, ALU.add))
                done("M", v.reciprocal(p12[:, 0:1], den2[:]))
                done("M", v.tensor_tensor(p12[:, 1:2], p12[:, 0:1], egap[:], ALU.mult))
                v.tensor_scalar(w1st[:], expert[:], idxf[:, 0:1], p12[:, 0:1], ALU.is_equal, ALU.mult)
                done("M", v.tensor_scalar(w2nd[:], expert[:], idxf[:, 1:2], p12[:, 1:2], ALU.is_equal, ALU.mult))
                done("M", v.tensor_tensor(wtok[:], w1st[:], w2nd[:], ALU.add))
                done("M", v.tensor_copy(wexp[:, 0:E], wtok[:]))
                done("M", v.tensor_tensor(wres[:], wtok[:], wexp[:, 0:E], ALU.subtract))
                done("M", v.tensor_copy(wexp[:, E:2 * E], wres[:]))
                v.tensor_tensor(wexp[:, 2 * E:3 * E], wres[:], wexp[:, E:2 * E], ALU.subtract).then_inc(wexp_ready, 1)

            def hidden(t, k):
                if not has_row("M", t):
                    return
                key = ("M", "gu", k)
                n = (FT // 2) * row_of("M", t) + k + 1
                two = slice(2 * k, 2 * k + 2)
                dve.wait_ge(th_ready, n)
                v.scalar_tensor_tensor(sg[:, two, :], th[:, two, :], 1.0, heads(bank(work, key)[:, 0:2 * P], P), ALU.add, ALU.mult).then_inc(sg_ready, 1)
                dve.wait_ge(sg_ready, n)
                v.tensor_tensor(su[:, two, :], sg[:, two, :], heads(bank(work, key)[:, 2 * P:4 * P], P), ALU.mult).then_inc(read_sem(work, key), 1)

            def keys_p(t):
                if has_row("P", t):
                    key = ("P", "kv")
                    dve.wait_ge(kh0_ready, row_of("P", t) + 1)
                    dve.wait_ge(v0_ready, row_of("P", t) + 1)
                    v.tensor_tensor(heads(kres[:], HD0), heads(bank(work, key)[:, 0:D], HD0),
                                    slots(kexp0, HD0)[:, :, 1, :], ALU.subtract).then_inc(read_sem(work, key), 1)

            def low_part(s, t, exp, hd, res, slot, middle, ready):
                if has_row(s, t):
                    dve.wait_ge(middle, row_of(s, t) + 1)
                    x = slots(exp, hd)
                    v.tensor_tensor(x[:, :, slot, :], heads(res[:], hd), x[:, :, 4, :], ALU.subtract).then_inc(ready, 1)

            def queries_p(t):
                if has_row("P", t):
                    key = ("P", "q")
                    dve.wait_ge(qh0_ready, row_of("P", t) + 1)
                    v.tensor_tensor(heads(qres0[:], HD0), heads(bank(work, key)[:, 0:D], HD0), slots(qexp0, HD0)[:, :, 0, :],
                                    ALU.subtract).then_inc(read_sem(work, key), 1)

            def keys_b(t):
                if has_row("B", t):
                    key = ("B", "kt")
                    wait_full(dve, work, key, t)
                    tiles = heads(bank(work, key)[:, 0:2 * P].bitcast(BF16), P)
                    for half in range(2):
                        rows = slice(half * L, (half + 1) * L)
                        last = v.tensor_copy(kz1[rows, half::2, :], tiles[rows])
                    last.then_inc(read_sem(work, key), 1)

            def end_a(t):
                if has_row("A", t):
                    key = ("A", "out")
                    wait_full(dve, near, key, t)
                    dve.wait_ge(xres_in, 16 * (row_of("A", t) + 1))
                    v.tensor_tensor(x1[:], xres[:], bank(near, key)[:, 0:D], ALU.add).then_inc(read_sem(near, key), 1)
                    wait_read(dve, near, key, t)
                    stats_of("A", x1)

            def end_m(t):
                if not has_row("M", t):
                    return
                key = ("M", "dn")
                wait_full(dve, work, key, t)
                v.tensor_tensor(x2[:], x1[:], bank(work, key)[:, 0:D], ALU.add).then_inc(read_sem(work, key), 1)
                wait_read(dve, work, key, t)
                stats_of("M", x2)

            def norm_m(t):
                if not has_row("M", t):
                    return
                r = row_of("M", t)
                dve.wait_ge(ln_rstd["M"], r + 1)
                src = x2[:].rearrange("p (u g j d) -> p u g j d", u=KV1 // 2, g=2, j=G1)
                dst = xhat["M"][:].rearrange("p (u j g d) -> p u j g d", u=KV1 // 2, g=2, j=G1)
                for g in range(2):
                    last = v.tensor_scalar(dst[:, :, :, g, :], src[:, :, g, :, :], mv["M"][:, 0:1], rstd["M"][:], ALU.subtract, ALU.mult)
                last.then_inc(xhat_ready["M"], 1)
                dve.wait_ge(xhat_ready["M"], r + 1)
                dve.wait_ge(qh1_ready, r + 1)
                v.tensor_tensor(heads(qres1[:], HD1), heads(xhat["M"][:], HD1), slots(qexp1, HD1)[:, :, 0, :],
                                ALU.subtract).then_inc(qres1_ready, 1)

            def dequantise():
                dve.wait_ge(ld_ffn, LD_FFN)
                dve.wait_ge(lora_copied, 8)
                for q, s in ((upq_sb, ups_sb), (dnq_sb, dns_sb)):
                    v.scalar_tensor_tensor(s[:], q[:], -7.5, s[:], ALU.add, ALU.mult).then_inc(deq_tmp, 1)
                dve.wait_ge(deq_tmp, 2)
                for w, s in ((upw, ups_sb), (dnw, dns_sb)):
                    v.tensor_tensor(w[:], w[:], s[:], ALU.add).then_inc(deq_ready, 1)

            for t in [kexp0, qexp0, mexp["A"], mexp["B"], kexp1, kz1, qexp1, wexp]:
                v.memset(t[:], 0.0).then_inc(zeroed_ready, 1)
            for t in [va0, va1]:
                v.memset(t[:], 1.0).then_inc(zeroed_ready, 1)
            for e in range(E):
                v.memset(expert[:, e:e + 1], float(e))
            dve.wait_ge(zeroed_ready, N_ZEROED)

            def body(t):
                now["t"] = t
                steps.update({s: 0 for s in LAG})
                norm_p(t)
                keys_b(t)
                copy_transposes(near, ("B", "qt", 0), qt1[:, 0:8, :], t)
                router(t)
                if has_row("P", t):
                    normalise("P", t, xin)
                    key = ("P", "ct")
                    wait_full(dve, work, key, t)
                    v.tensor_copy(ct[:], bank(work, key)[0:L, 0:P]).then_inc(read_sem(work, key), 1)
                router_weights(t)
                maximum("B", t, 0)
                hidden(t, 0)
                maximum("B", t, 1)
                keys_p(t)
                maximum("B", t, 2)
                maximum("B", t, 3)
                low_part("P", t, kexp0, HD0, kres, 0, km0_ready, kexp0_ready)
                maximum("B", t, 4)
                hidden(t, 1)
                maximum("B", t, 5)
                queries_p(t)
                copy_transposes(work, ("P", "kt", 0), kt0[:, 0:8, :], t)
                maximum("B", t, 6)
                low_part("P", t, qexp0, HD0, qres0, 5, qm0_ready, qexp0_ready)
                maximum("B", t, 7)
                maximum_parts("B", t)
                copy_maxima("B", t)
                hidden(t, 2)
                copy_transposes(work, ("P", "qt", 0), qt0[:, 0:8, :], t)
                maximum("A", t, 0)
                if has_row("M", t):
                    key = ("M", "wt")
                    wait_full(dve, work, key, t)
                    v.tensor_copy(wt[:], bank(work, key)[:, 0:P // 2].bitcast(BF16)).then_inc(read_sem(work, key), 1)
                for k in range(1, N0):
                    maximum("A", t, k)
                maximum_parts("A", t)
                copy_maxima("A", t)
                if isinstance(t, int) and t == 1:
                    dequantise()
                if has_row("B", t):
                    attended("B", t)
                    r = row_of("B", t)
                    dve.wait_ge(ao_ready["B"], r + 1)
                    v.tensor_tensor(x3[:], x2[:], ao["B"][:], ALU.add).then_inc(x3_ready, 1)
                    dve.wait_ge(x3_ready, r + 1)
                    stats_of("B", x3)
                    normalise("B", t, x3)
                end_m(t)
                norm_m(t)
                low_part("M", t, qexp1, HD1, qres1, 5, qm1_ready, qexp1_ready)
                if has_row("A", t):
                    attended("A", t)
                end_a(t)
                if has_row("A", t):
                    normalise("A", t, x1)
                if has_row("F", t):
                    key = ("F", "fd")
                    r = row_of("F", t)
                    wait_full(dve, work, key, t)
                    dve.wait_ge(xb_ready, r + 1)
                    wait_at_least(dve, stored, 16 * r)
                    v.tensor_tensor(xo[:], xb[:], bank(work, key)[:, 0:D], ALU.add).then_inc(read_sem(work, key), 1)
                assert all(steps[s] == VSTEPS[s] for s in LAG if has_row(s, t)), steps

            pipeline(dve, body)

        @block.tensor
        def _(pe):
            m = nc.tensor

            def lora():
                pe.wait_ge(ld_lora, 64)
                for b in range(4):
                    m.matmul(lora_banks[b][:], upa_sb[:, (b // 2) * P:(b // 2 + 1) * P], upb_sb[:, (b % 2) * 512:(b % 2 + 1) * 512],
                             start=True, stop=True).then_inc(lora_mm, 1)
                for b in range(4):
                    if b >= 2:
                        pe.wait_ge(lora_copied, b - 1)
                    for c in range(2):
                        last = m.matmul(lora_banks[4 + b][:, c * D:(c + 1) * D], dna_sb[:, (2 * b + c) * P:(2 * b + c + 1) * P], dnb_sb[:],
                                        start=True, stop=True)
                    last.then_inc(lora_mm, 1)

            def transpose_rows(ring, key, src, t, chunks):
                wait_free(pe, ring, key, t)
                for n, c in enumerate(chunks):
                    last = m.transpose(bank(ring, key)[:, n * P:(n + 1) * P], src[:, c * P:(c + 1) * P], idf[:])
                last.then_inc(ring.full, 1)

            def transpose_tiles(ring, key, tiles, t):
                wait_free(pe, ring, key, t)
                to = bank(ring, key)[:].bitcast(BF16)
                for k, tile in enumerate(tiles):
                    last = m.transpose(to[:, k * P:(k + 1) * P], tile, idb[:])
                last.then_inc(ring.full, 1)

            def product(ring, key, t, left, right, chunks, width=D):
                wait_free(pe, ring, key, t)
                for c in range(chunks):
                    last = m.matmul(bank(ring, key)[:, 0:width], left[:, c, :], right[:, c, :], start=c == 0, stop=c == chunks - 1)
                last.then_inc(ring.full, 1)

            def natural(s, t, k):
                if not has_row(s, t):
                    return
                key = (s, "nat", k)
                wait_free(pe, near, key, t)
                to = bank(near, key)
                if s == "B":
                    if k == 0:
                        wait_read(pe, work, ("B", "kt"), t)
                    if k % 4 == 0:
                        wait_read(pe, near, ("B", "qt", k // 4), t)
                    u = k // 2
                    for jj in range(2):
                        j = 2 * (k % 2) + jj
                        last = m.matmul(to[:, jj * 2 * P:(jj + 1) * 2 * P], qt1[:, 4 * u + j, :], kz1[:, 2 * u:2 * u + 2, :],
                                        start=True, stop=True)
                else:
                    if k == 0:
                        for n in range(2):
                            wait_read(pe, work, ("P", "kt", n), t)
                            wait_read(pe, work, ("P", "qt", n), t)
                    m.matmul(to[:], idb[:], maskq[:], start=True, stop=False, skip_group_check=True)
                    for j in range(4):
                        h = 4 * k + j
                        last = m.matmul(to[:, j * P:(j + 1) * P], qt0[:, h, :], kt0[:, h, :], start=False, stop=True,
                                        skip_group_check=True)
                last.then_inc(near.full, 1)

            def transpose_maxima(s, t):
                if has_row(s, t):
                    pe.wait_ge(mexp_ready[s], row_of(s, t) + 1)
                    transpose_tiles(near, (s, "mt"), [mexp[s][:, j, :] for j in range(G1)], t)

            def shifted(s, t, k):
                if not has_row(s, t):
                    return
                key = (s, "s", k)
                wait_at_least(pe, exp_ready, far.before(key, t) - 1)
                if k == 0:
                    wait_read(pe, near, (s, "mt"), t)
                to = ps_far[far.bank(key)]
                if s == "B":
                    m.matmul(to[:], selg[:, k, :], mt[s][:], start=True, stop=False)
                    last = m.matmul(to[:], kz1[:, k, :], qt1[:, 4 * (k // 2):4 * (k // 2) + 4, :], start=False, stop=True)
                else:
                    m.matmul(to[:], idb[:], maskk[:], start=True, stop=False, skip_group_check=True)
                    m.matmul(to[:], selg[:, k, :], mt[s][:], start=False, stop=False, skip_group_check=True)
                    for j in range(4):
                        h = 4 * k + j
                        last = m.matmul(to[:, j * P:(j + 1) * P], kt0[:, h, :], qt0[:, h, :], start=False, stop=True,
                                        skip_group_check=True)
                last.then_inc(far.full, 1)

            def weigh_values(s, t, k):
                if not has_row(s, t):
                    return
                key = (s, "s", k)
                r = row_of(s, t)
                pe.wait_ge(exp_ready, far.before(key, t) + 1)
                if k == 0:
                    wait_at_least(pe, ao_ready[s], r)
                    pe.wait_ge(v1_ready if s == "B" else v0_ready, r + 1)
                w = (HD1 if s == "B" else HD0) + 1
                for j in range(4):
                    h = 4 * k + j
                    value = va1[:, k, :] if s == "B" else va0[:, h, :]
                    last = m.matmul(ps_pv[s][:, h * w:(h + 1) * w], pt[far.order.index(key) % NPT][:, j, :], value, start=True, stop=True)
                last.then_inc(pv_done, 1)

            def gate_up(t, k):
                if not has_row("M", t):
                    return
                key = ("M", "gu", k)
                if isinstance(t, int):
                    pe.wait_ge(ld_moe, 48)
                wait_free(pe, work, key, t)
                for n, w in enumerate((wg_sb, wu_sb)):
                    for tile in range(2):
                        f = 2 * k + tile
                        for c in range(DC):
                            last = m.matmul(bank(work, key)[:, (2 * n + tile) * P:(2 * n + tile + 1) * P], w[:, c, f * P:(f + 1) * P], xht1[:, c, :],
                                            start=c == 0, stop=c == DC - 1)
                last.then_inc(work.full, 1)

            def up(t, k):
                if not has_row("F", t):
                    return
                key = ("F", "up", k)
                wait_read(pe, work, ("F", "xt"), t)
                if isinstance(t, int):
                    pe.wait_ge(deq_ready, 2)
                wait_free(pe, work, key, t)
                for n in range(4):
                    h = 4 * k + n
                    for c in range(DC):
                        last = m.matmul(bank(work, key)[:, n * P:(n + 1) * P], upw[:, c, h * P:(h + 1) * P], xht3[:, c, :],
                                        start=c == 0, stop=c == DC - 1)
                last.then_inc(work.full, 1)

            def weights_spread(t, k):
                if not has_row("M", t):
                    return
                key = ("M", "wb", k)
                wait_read(pe, work, ("M", "wt"), t)
                wait_free(pe, work, key, t)
                sel = sele[:].rearrange("p e f -> p (e f)")
                for n in range(4 if k == 0 else FT - 4):
                    f = 4 * k + n
                    last = m.matmul(bank(work, key)[:, n * P:(n + 1) * P], sel[:, f * P:(f + 1) * P], wt[:], start=True, stop=True)
                last.then_inc(work.full, 1)

            def transpose_queries_p(t, c):
                if has_row("P", t):
                    pe.wait_ge(qexp0_ready, row_of("P", t) + 1)
                    transpose_tiles(work, ("P", "qt", c), [qexp0[:, 8 * c + k, :] for k in range(8)], t)

            def transpose_keys_p(t, c):
                if has_row("P", t):
                    pe.wait_ge(kexp0_ready, row_of("P", t) + 1)
                    transpose_tiles(work, ("P", "kt", c), [kexp0[:, 8 * c + k, :] for k in range(8)], t)

            def body(t):
                f, mm, b, a_, p_ = (has_row(s, t) for s in ("F", "M", "B", "A", "P"))
                if mm:
                    pe.wait_ge(xhat_ready["A"], row_of("M", t) + 1)
                    transpose_rows(work, ("M", "xt"), xhat["A"], t, range(DC))
                if b:
                    pe.wait_ge(qexp1_ready, row_of("B", t) + 1)
                    for c in range(2):
                        transpose_tiles(near, ("B", "qt", c), [qexp1[:, 2 * k:2 * k + 2, :].rearrange("p h s -> p (h s)") for k in range(8 * c, 8 * c + 8)], t)
                    pe.wait_ge(kexp1_ready, row_of("B", t) + 1)
                    transpose_tiles(work, ("B", "kt"), [kexp1[:, 2 * u:2 * u + 2, :].rearrange("p g s -> p (g s)") for u in range(KV1 // 2)], t)
                if mm:
                    if isinstance(t, int):
                        pe.wait_ge(ld_moe, 48)
                    wait_read(pe, work, ("M", "xt"), t)
                    product(work, ("M", "rt"), t, xht1, wr_sb, DC, E)
                if p_:
                    key = ("P", "ct")
                    pe.wait_ge(c_in, 16 * (row_of("P", t) + 1))
                    wait_free(pe, work, key, t)
                    detach(pe)
                    m.transpose(bank(work, key)[0:L, 0:P], cin[:], idf[:]).then_inc(work.full, 1)
                gate_up(t, 0)
                natural("B", t, 0)
                natural("B", t, 1)
                if p_:
                    key = ("P", "kv")
                    if isinstance(t, int):
                        pe.wait_ge(ld_kv, 16)
                    wait_read(pe, work, ("P", "ct"), t)
                    wait_free(pe, work, key, t)
                    m.matmul(bank(work, key)[:], ct[:], wkv_sb[:], start=True, stop=True).then_inc(work.full, 1)
                natural("B", t, 2)
                if p_:
                    pe.wait_ge(xhat_ready["P"], row_of("P", t) + 1)
                    transpose_rows(work, ("P", "xt"), xhat["P"], t, range(DC))
                natural("B", t, 3)
                gate_up(t, 1)
                natural("B", t, 4)
                if p_:
                    if isinstance(t, int):
                        pe.wait_ge(ld_q, 16)
                    wait_read(pe, work, ("P", "xt"), t)
                    product(work, ("P", "q"), t, xht0, wq_sb, DC)
                natural("B", t, 5)
                natural("B", t, 6)
                transpose_keys_p(t, 0)
                transpose_keys_p(t, 1)
                natural("B", t, 7)
                gate_up(t, 2)
                transpose_maxima("B", t)
                transpose_queries_p(t, 0)
                shifted("B", t, 0)
                shifted("B", t, 1)
                transpose_queries_p(t, 1)
                for k in range(N0):
                    weigh_values("B", t, k)
                    shifted("B", t, k + 2)
                    natural("A", t, k)
                    if mm and k == 0:
                        pe.wait_ge(wexp_ready, row_of("M", t) + 1)
                        transpose_tiles(work, ("M", "wt"), [wexp[:]], t)
                    if k >= 2:
                        weights_spread(t, k - 2)
                weigh_values("B", t, 4)
                shifted("B", t, 6)
                weigh_values("B", t, 5)
                shifted("B", t, 7)
                transpose_maxima("A", t)
                weigh_values("B", t, 6)
                shifted("A", t, 0)
                weigh_values("B", t, 7)
                shifted("A", t, 1)
                weigh_values("A", t, 0)
                shifted("A", t, 2)
                if mm:
                    if isinstance(t, int):
                        pe.wait_ge(ld_down, 16)
                    pe.wait_ge(hid_ready, (FT // 2) * (row_of("M", t) + 1))
                    product(work, ("M", "dn"), t, hid, wd_sb, FT)
                if f:
                    pe.wait_ge(xhat_ready["B"], row_of("F", t) + 1)
                    transpose_rows(work, ("F", "xt"), xhat["B"], t, range(DC))
                weigh_values("A", t, 1)
                shifted("A", t, 3)
                up(t, 0)
                weigh_values("A", t, 2)
                weigh_values("A", t, 3)
                up(t, 1)
                if a_:
                    pe.wait_ge(ao_ready["A"], row_of("A", t) + 1)
                    transpose_rows(near, ("A", "at"), ao["A"], t, range(DC))
                    if isinstance(t, int):
                        pe.wait_ge(ld_out, 16)
                    wait_read(pe, near, ("A", "at"), t)
                    product(near, ("A", "out"), t, aot, wout_sb, DC)
                if f:
                    for k in range(2):
                        wait_read(pe, work, ("F", "up", k), t)
                    product(work, ("F", "fd"), t, hft, dnw, HT)

            lora()
            pe.wait_ge(ident_ready, 2)
            pe.wait_ge(lora_copied, 8)
            pe.wait_ge(const_ready, N_CONST)
            pipeline(pe, body)

    return nc


_INS = ["x", "ctx", "wq", "wkv", "wout", "wr", "wg", "wu", "wd", "upq", "ups", "bup", "upa", "upb", "dnq", "dns", "bdn", "dna", "dnb"]


def kernel(x, ctx_512, L0_xattn_Wq, L0_xattn_Wkv_expand, L0_xattn_Wout, L0_ffn_w_gate_router, L0_ffn_w_gate_proj,
           L0_ffn_w_up_proj, L0_ffn_w_down_proj, L1_ffn_w_up_q, L1_ffn_w_up_scale, L1_ffn_b_up, L1_ffn_w_up_lora_a,
           L1_ffn_w_up_lora_b, L1_ffn_w_down_q, L1_ffn_w_down_scale, L1_ffn_b_down, L1_ffn_w_down_lora_a, L1_ffn_w_down_lora_b):
    import numpy as np
    import concourse.bacc as bacc
    from concourse.bass_utils import run_bass_kernel_spmd

    laid = {
        "x": np.asarray(x), "ctx": np.asarray(ctx_512),
        "wq": np.asarray(L0_xattn_Wq).T, "wkv": np.asarray(L0_xattn_Wkv_expand).T, "wout": np.asarray(L0_xattn_Wout).T,
        "wr": np.asarray(L0_ffn_w_gate_router).T,
        "wg": np.asarray(L0_ffn_w_gate_proj).reshape(E * F, D).T, "wu": np.asarray(L0_ffn_w_up_proj).reshape(E * F, D).T,
        "wd": np.asarray(L0_ffn_w_down_proj).transpose(0, 2, 1).reshape(E * F, D),
        "upq": np.asarray(L1_ffn_w_up_q).T, "ups": np.asarray(L1_ffn_w_up_scale).T,
        "bup": np.asarray(L1_ffn_b_up).reshape(HT, P).T,
        "upa": np.asarray(L1_ffn_w_up_lora_a).T, "upb": np.asarray(L1_ffn_w_up_lora_b),
        "dnq": np.asarray(L1_ffn_w_down_q).T, "dns": np.asarray(L1_ffn_w_down_scale).T,
        "bdn": np.asarray(L1_ffn_b_down).reshape(1, D),
        "dna": np.asarray(L1_ffn_w_down_lora_a).T, "dnb": np.asarray(L1_ffn_w_down_lora_b),
    }
    nc = bacc.Bacc("TRN2", target_bir_lowering=False, num_devices=1)
    arrays, args = {}, []
    for name in _INS:
        a = np.ascontiguousarray(laid[name])
        arrays[f"in_{name}_dram"] = a
        args.append(nc.dram_tensor(f"in_{name}_dram", a.shape, mybir.dt.from_np(a.dtype), kind="ExternalInput").ap())
    out = nc.dram_tensor("out_dram", laid["x"].shape, F32, kind="ExternalOutput").ap()
    build(nc, *args, out)
    r = run_bass_kernel_spmd(nc, [arrays], core_ids=[0])
    return r.results[0]["out_dram"]
```

```python
from contextlib import ExitStack

import concourse.bass as bass
from concourse import mybir

F32 = mybir.dt.float32
BF16 = mybir.dt.bfloat16
I32 = mybir.dt.int32
U32 = mybir.dt.uint32
ALU = mybir.AluOpType
ACT = mybir.ActivationFunctionType
AX_X = mybir.AxisListType.X

P = 128
D = 256
DC = D // P
L = 64
NH0, HD0 = 16, 16
NH1, KV1, HD1 = 32, 8, 8
G1 = NH1 // KV1
E, F = 8, 96
FT = E * F // P
H = 1024
HT = H // P
R = 16
BLOCK = 64
W0 = NH0 * (HD0 + 1)
W1 = NH1 * (HD1 + 1)
EPS = 1e-5
MASKED = -1e30
TERMS = 6



LAG = {"P": 0,
       "A": 0,
       "M": 1,
       "K": 1,
       "B": 2,
       "F": 2,
       "G": 3}
DEPTH = max(LAG.values())


class Uses:

    def __init__(self, order, banks, rows):
        self.order, self.banks, self.rows = order, banks, rows

    def active(self, key, t):
        return 0 <= t - LAG[key[0]] < self.rows

    def bank(self, key):
        return self.order.index(key) % self.banks

    def before(self, key, t, bank=None):
        mine = [k for k in self.order if bank is None or self.bank(k) == bank]
        if not isinstance(t, int):
            return self.before(key, DEPTH, bank) + (t - DEPTH) * len(mine)
        n = sum(self.active(k, u) for u in range(t) for k in mine)
        return n + sum(self.active(k, t) for k in mine if self.order.index(k) < self.order.index(key))

    def at_start(self, t, bank):
        mine = [k for k in self.order if self.bank(k) == bank]
        if not isinstance(t, int):
            return self.at_start(DEPTH, bank) + (t - DEPTH) * len(mine)
        return sum(self.active(k, u) for u in range(t) for k in mine)


def build(nc, x, ctx, wq, wkv, wout, wr, wg, wu, wd, upq, ups, bup, upa, upb, dnq, dns, bdn, dna, dnb, out):
    ROWS = x.shape[0]
    N0, N1 = NH0 // 4, NH1 // 4
    NPT = 4

    work = Uses([("M", "xt"), ("B", "kt"), ("M", "rt"), ("P", "ct"), ("M", "gu", 0), ("P", "kv"), ("P", "xt"), ("M", "gu", 1),
                 ("P", "q"), ("P", "kt", 0), ("P", "kt", 1), ("M", "gu", 2), ("P", "qt", 0), ("P", "qt", 1), ("M", "wt"),
                 ("M", "wb", 0), ("M", "wb", 1), ("M", "dn"), ("F", "xt"), ("F", "up", 0), ("F", "up", 1)], 2, ROWS)
    near = Uses([("B", "qt", 0), ("B", "qt", 1)] + [("B", "nat", k) for k in range(N1)] + [("B", "mt")]
                + [("A", "nat", k) for k in range(N0)] + [("A", "mt"), ("A", "at"), ("A", "out")], 2, ROWS)
    far = Uses([("B", "s", k) for k in range(N1)] + [("A", "s", k) for k in range(N0)], 2, ROWS)

    with ExitStack() as stack:
        def sb(name, shape, dt=F32):
            return stack.enter_context(nc.sbuf_tensor(name, shape, dt))

        def psum(name, shape, dt=F32):
            return stack.enter_context(nc.psum_tensor(name, shape, dt))

        def sem(name):
            return stack.enter_context(nc.semaphore(name))

        def sems(name, n=2):
            return [sem(f"{name}{k}") for k in range(n)]

        wq_sb = sb("wq_sb", [P, DC, D])
        wkv_sb = sb("wkv_sb", [L, 2 * D])
        wout_sb = sb("wout_sb", [P, DC, D])
        wr_sb = sb("wr_sb", [P, DC, E])
        wg_sb = sb("wg_sb", [P, DC, E * F])
        wu_sb = sb("wu_sb", [P, DC, E * F])
        wd_sb = sb("wd_sb", [P, FT, D])
        upq_sb = sb("upq_sb", [P, DC, H], I32)
        dnq_sb = sb("dnq_sb", [P, HT, D], I32)
        ups_sb = sb("ups_sb", [P, DC, H])
        dns_sb = sb("dns_sb", [P, HT, D])
        upw = sb("upw", [P, DC, H])
        dnw = sb("dnw", [P, HT, D])
        bup_sb = sb("bup_sb", [P, HT])
        bdn_sb = sb("bdn_sb", [P, D])
        upa_sb = sb("upa_sb", [R, D])
        upb_sb = sb("upb_sb", [R, H])
        dna_sb = sb("dna_sb", [R, H])
        dnb_sb = sb("dnb_sb", [R, D])
        idf = sb("idf", [P, P])
        idb = sb("idb", [P, P], BF16)
        maskq = sb("maskq", [P, 4, P], BF16)
        maskk = sb("maskk", [P, 4, P], BF16)
        selg = sb("selg", [P, KV1, P], BF16)
        sele = sb("sele", [P, E, F], BF16)
        mhalf = sb("mhalf", [P, 1])
        expert = sb("expert", [P, E])
        minus_one = sb("minus_one", [P, 1])
        cin = sb("cin", [P, L])
        xin = sb("xin", [P, D])
        ct = sb("ct", [L, P])
        kres = sb("kres", [P, D])
        kexp0 = sb("kexp0", [P, NH0, P], BF16)
        qres0 = sb("qres0", [P, D])
        qexp0 = sb("qexp0", [P, NH0, P], BF16)
        xht0 = sb("xht0", [P, DC, P])
        kt0 = sb("kt0", [P, NH0, P], BF16)
        qt0 = sb("qt0", [P, NH0, P], BF16)
        va0 = sb("va0", [P, NH0, HD0 + 1])
        norms = ("P", "A", "M", "B")
        stats = {s: sb(f"stats{s}", [P, 6]) for s in norms}
        mv = {s: sb(f"mv{s}", [P, 2]) for s in norms}
        var_eps = {s: sb(f"var_eps{s}", [P, 1]) for s in norms}
        rstd = {s: sb(f"rstd{s}", [P, 1]) for s in norms}
        xhat = {s: sb(f"xhat{s}", [P, D]) for s in norms}
        nmax = {s: sb(f"nmax{s}", [P, G1, KV1]) for s in "AB"}
        mexp = {s: sb(f"mexp{s}", [P, G1, P], BF16) for s in "AB"}
        mt = {s: sb(f"mt{s}", [P, G1 * P], BF16) for s in "AB"}
        pt = [sb(f"pt{k}", [P, 4, P]) for k in range(NPT)]
        rden = {s: sb(f"rden{s}", [P, NH1]) for s in "AB"}
        ao = {s: sb(f"ao{s}", [P, D]) for s in "AB"}
        aot = sb("aot", [P, DC, P])
        xres = sb("xres", [P, D])
        x1 = sb("x1", [P, D])
        xht1 = sb("xht1", [P, DC, P])
        score = sb("score", [P, E])
        top8 = sb("top8", [P, 8])
        idx8 = sb("idx8", [P, 8], U32)
        idxf = sb("idxf", [P, 2])
        gap = sb("gap", [P, 1])
        egap = sb("egap", [P, 1])
        den2 = sb("den2", [P, 1])
        p12 = sb("p12", [P, 2])
        w1st = sb("w1st", [P, E])
        w2nd = sb("w2nd", [P, E])
        wtok = sb("wtok", [P, E])
        wres = sb("wres", [P, E])
        wexp = sb("wexp", [P, P], BF16)
        wt = sb("wt", [P, P], BF16)
        wb = sb("wb", [P, FT, P])
        th = sb("th", [P, FT, P])
        sg = sb("sg", [P, FT, P])
        su = sb("su", [P, FT, P])
        hid = sb("hid", [P, FT, P])
        x2 = sb("x2", [P, D])
        qres1 = sb("qres1", [P, D])
        qexp1 = sb("qexp1", [P, NH1, L], BF16)
        cinb = sb("cinb", [P, L])
        kres1 = sb("kres1", [P, L])
        kexp1 = sb("kexp1", [P, KV1, L], BF16)
        kz1 = sb("kz1", [P, KV1, P], BF16)
        va1 = sb("va1", [P, KV1, HD1 + 1])
        qt1 = sb("qt1", [P, NH1 // 2, P], BF16)
        x3 = sb("x3", [P, D])
        xb = sb("xb", [P, D])
        xht3 = sb("xht3", [P, DC, P])
        hft = sb("hft", [P, HT, P])
        xo = sb("xo", [P, D])

        ps_work = [psum(f"ps_work{k}", [P, 512]) for k in range(2)]
        ps_near = [psum(f"ps_near{k}", [P, 512]) for k in range(2)]
        ps_far = [psum(f"ps_far{k}", [P, 512]) for k in range(2)]
        ps_pv = {s: psum(f"ps_pv{s}", [P, 512]) for s in "AB"}
        ps_lora = ps_pv["B"]

        c_in, x_in, xres_in, cinb_in = sem("c_in"), sem("x_in"), sem("xres_in"), sem("cinb_in")
        ld_kv, ld_q, ld_out, ld_moe, ld_down, ld_lora, ld_ffn = (sem(f"ld_{n}") for n in
                                                                 ("kv", "q", "out", "moe", "down", "lora", "ffn"))
        stored = sem("stored")
        pool_set, ident_ready, const_ready, zeroed_ready = sem("pool_set"), sem("ident_ready"), sem("const_ready"), sem("zeroed_ready")
        lora_mm, lora_copied = sem("lora_mm"), sem("lora_copied")
        deq_tmp, deq_ready = sem("deq_tmp"), sem("deq_ready")
        work.full, work.read, work.ps = sem("work_full"), sems("work_read"), ps_work
        near.full, near.read, near.ps = sem("near_full"), sems("near_read"), ps_near
        far.full, exp_ready, pv_done = sem("far_full"), sem("exp_ready"), sem("pv_done")
        ln_var, ln_pool, ln_rstd, xhat_ready = ({s: sem(f"{n}{s}") for s in norms} for n in
                                                ("ln_var", "ln_pool", "ln_rstd", "xhat_ready"))
        v0_ready, kh0_ready, km0_ready, kexp0_ready = sem("v0_ready"), sem("kh0_ready"), sem("km0_ready"), sem("kexp0_ready")
        v1_ready, kh1_ready, kres1_ready, km1_ready, kexp1_ready = (sem(n) for n in (
            "v1_ready", "kh1_ready", "kres1_ready", "km1_ready", "kexp1_ready"))
        qh0_ready, qm0_ready, qexp0_ready = sem("qh0_ready"), sem("qm0_ready"), sem("qexp0_ready")
        qh1_ready, qres1_ready, qm1_ready, qexp1_ready = sem("qh1_ready"), sem("qres1_ready"), sem("qm1_ready"), sem("qexp1_ready")
        mhigh_ready, mexp_ready, ao_ready = ({s: sem(f"{n}{s}") for s in "AB"} for n in ("mhigh_ready", "mexp_ready", "ao_ready"))
        x3_ready, xb_ready = sem("x3_ready"), sem("xb_ready")
        down_full, xo_ready = sem("down_full"), sem("xo_ready")
        gap_ready, egap_ready, idx_ready, wexp_ready = sem("gap_ready"), sem("egap_ready"), sem("idx_ready"), sem("wexp_ready")
        share_step = sem("share_step")
        th_ready, sg_ready, hid_ready = sem("th_ready"), sem("sg_ready"), sem("hid_ready")
        vstep = {s: sem(f"vstep{s}") for s in LAG}

        block = stack.enter_context(nc.Block())
        LD_FFN = 16 * 10
        VSTEPS = {"P": 1, "A": 2, "M": 3, "K": 0, "B": 2, "F": 0, "G": 0}
        LORA_BODY = 1
        N_CONST, N_ZEROED, N_LORA, SHARE_STEPS = 7, 11 + E, 8, 9

        def wait_at_least(eng, s, count):
            if not isinstance(count, int) or count > 0:
                eng.wait_ge(s, count)

        def detach(eng):
            eng.nop(nofuse=True)

        def bank(ring, key):
            return ring.ps[ring.bank(key)]

        def read_sem(ring, key):
            return ring.read[ring.bank(key)]

        def wait_free(eng, ring, key, t):
            wait_at_least(eng, read_sem(ring, key), ring.before(key, t, ring.bank(key)))

        def wait_full(eng, ring, key, t):
            eng.wait_ge(ring.full, ring.before(key, t) + 1)

        def wait_read(eng, ring, key, t):
            eng.wait_ge(read_sem(ring, key), ring.before(key, t, ring.bank(key)) + 1)

        def row_of(stage, t):
            return t - LAG[stage]

        def has_row(stage, t):
            return not isinstance(t, int) or 0 <= row_of(stage, t) < ROWS

        def pipeline(eng, body):
            for t in range(DEPTH):
                body(t)
            with eng.Fori(DEPTH, ROWS) as t:
                body(t)
            for t in range(ROWS, ROWS + DEPTH):
                body(t)

        def heads(ap, hd):
            return ap.rearrange("p (h d) -> p h d", d=hd)

        def slots(exp, hd):
            return exp[:, :, 0:TERMS * hd].rearrange("p h (s d) -> p h s d", d=hd)

        def repeated(ap, n, hd):
            return ap.rearrange("p (h s d) -> p h s d", s=1, d=hd).broadcast_to([P, ap.shape[1] // hd, n, hd])

        def dram_row(ap, r):
            return ap[bass.ds(r, 1), :, :].rearrange("a t c -> t (a c)")

        @block.sync
        def _(sp):
            def weights():
                sp.dma_start(wout_sb[:], wout.rearrange("(c p) n -> p c n", p=P)).then_inc(ld_out, 16)
                sp.dma_start(wr_sb[:], wr.rearrange("(c p) n -> p c n", p=P)).then_inc(ld_moe, 16)
                sp.dma_start(wg_sb[:], wg.rearrange("(c p) n -> p c n", p=P)).then_inc(ld_moe, 16)
                sp.dma_start(wu_sb[:], wu.rearrange("(c p) n -> p c n", p=P)).then_inc(ld_moe, 16)
                sp.dma_start(wd_sb[:], wd.rearrange("(c p) n -> p c n", p=P)).then_inc(ld_down, 16)
                for c in range(DC):
                    for half in range(2):
                        sp.dma_start(ups_sb[half * BLOCK:(half + 1) * BLOCK, c, :],
                                     ups[2 * c + half:2 * c + half + 1, :].broadcast_to([BLOCK, H])).then_inc(ld_ffn, 16)
                for half in range(2):
                    sp.dma_start(dns_sb[half * BLOCK:(half + 1) * BLOCK, :, :],
                                 dns.rearrange("(c a) n -> a c n", a=2)[half:half + 1, :, :].broadcast_to([BLOCK, HT, D])).then_inc(ld_ffn, 16)
                sp.dma_start(upq_sb[:], upq.rearrange("(c p) n -> p c n", p=P)).then_inc(ld_ffn, 16)
                sp.dma_start(dnq_sb[:], dnq.rearrange("(c p) n -> p c n", p=P)).then_inc(ld_ffn, 16)
                sp.dma_start(bup_sb[:], bup).then_inc(ld_ffn, 16)
                sp.dma_start(bdn_sb[:], bdn.broadcast_to([P, D])).then_inc(ld_ffn, 16)

            def body(t):
                if has_row("P", t):
                    r = row_of("P", t)
                    if not isinstance(t, int) or t > 0:
                        sp.wait_ge(v0_ready, r)
                        sp.wait_ge(xhat_ready["P"], r)
                    sp.dma_start(cin[:], dram_row(ctx, r)).then_inc(c_in, 16)
                    sp.dma_start(xin[:], dram_row(x, r)).then_inc(x_in, 16)
                if isinstance(t, int) and t == 0:
                    sp.dma_start(wkv_sb[:], wkv).then_inc(ld_kv, 16)
                    sp.dma_start(wq_sb[:], wq.rearrange("(c p) n -> p c n", p=P)).then_inc(ld_q, 16)
                if has_row("A", t):
                    r = row_of("A", t)
                    if not isinstance(t, int) or r > 0:
                        sp.wait_ge(ln_var["A"], r)
                    sp.dma_start(xres[:], dram_row(x, r)).then_inc(xres_in, 16)
                if isinstance(t, int) and t == 0:
                    weights()
                if has_row("K", t):
                    r = row_of("K", t)
                    if not isinstance(t, int) or r > 0:
                        sp.wait_ge(kexp1_ready, r)
                        sp.wait_ge(v1_ready, r)
                    sp.dma_start(cinb[:], dram_row(ctx, r)).then_inc(cinb_in, 16)
                if has_row("G", t):
                    r = row_of("G", t)
                    sp.wait_ge(xo_ready, r + 1)
                    sp.dma_start(dram_row(out, r), xo[:]).then_inc(stored, 16)

            pipeline(sp, body)
            sp.wait_ge(stored, 16 * ROWS)

        @block.gpsimd
        def _(pool):
            g = nc.gpsimd
            def zero(tensors):
                for t in tensors:
                    g.memset(t[:], 0.0).then_inc(pool_set, 1)

            def fill(t, value, pattern, base, cm, op=ALU.not_equal, ready=const_ready):
                g.affine_select(out=t, in_=t, compare_op=op, fill=value, base=base, pattern=pattern,
                                channel_multiplier=cm).then_inc(ready, 1)

            def constants():
                zero([maskq, maskk, selg, sele])
                pool.wait_ge(pool_set, 7)
                fill(maskq[:], MASKED, [[0, 4], [-1, P]], 0, 1, ALU.is_ge)
                fill(maskk[:], MASKED, [[0, 4], [1, P]], 0, -1, ALU.is_ge)
                fill(selg[:], 1.0, [[-1, KV1], [0, P]], 0, 1)
                fill(sele[:], 0.5, [[-1, E], [0, F]], 0, 1)
                pool.wait_ge(const_ready, 4)
                fill(selg[:], 1.0, [[-1, KV1], [0, P]], -KV1, 1)
                fill(sele[:], 0.5, [[-1, E], [0, F]], -E, 1)
                pool.wait_ge(const_ready, 6)
                fill(sele[:], 0.5, [[-1, E], [0, F]], -2 * E, 1)

            zero([idf, idb])
            pool.wait_ge(pool_set, 2)
            fill(idf[:], 1.0, [[-1, P]], 0, 1, ready=ident_ready)
            fill(idb[:], 1.0, [[-1, P]], 0, 1, ready=ident_ready)
            g.memset(mhalf[:], -0.5).then_inc(pool_set, 1)
            pool.wait_ge(pool_set, 3)

            def layernorm_rstd(s, t):
                if not has_row(s, t):
                    return
                r = row_of(s, t)
                pool.wait_ge(ln_var[s], r + 1)
                detach(pool)
                g.tensor_scalar(var_eps[s][:], mv[s][:, 1:2], EPS, None, ALU.add).then_inc(ln_pool[s], 1)
                pool.wait_ge(ln_pool[s], r + 1)
                g.tensor_tensor(rstd[s][:], var_eps[s][:], mhalf[:], ALU.pow).then_inc(ln_rstd[s], 1)

            def key_parts(t):
                if not has_row("K", t):
                    return
                r = row_of("K", t)
                pool.wait_ge(kh1_ready, r + 1)
                k1 = slots(kexp1, HD1)
                res = heads(kres1[:], HD1)
                g.tensor_tensor(res, heads(cinb[:], HD1), k1[:, :, 1, :], ALU.subtract).then_inc(kres1_ready, 1)
                pool.wait_ge(kres1_ready, r + 1)
                detach(pool)
                g.tensor_copy(k1[:, :, 2:5:2, :], repeated(kres1[:], 2, HD1)).then_inc(km1_ready, 1)
                pool.wait_ge(km1_ready, r + 1)
                g.tensor_tensor(k1[:, :, 0, :], res, k1[:, :, 2, :], ALU.subtract).then_inc(kexp1_ready, 1)

            def values(t):
                if not has_row("K", t):
                    return
                r = row_of("K", t)
                pool.wait_ge(cinb_in, 16 * (r + 1))
                wait_at_least(pool, ao_ready["B"], r)
                detach(pool)
                g.tensor_copy(va1[:, :, 0:HD1], heads(cinb[:], HD1)).then_inc(v1_ready, 1)

            def hidden_weighed(t, k):
                if not has_row("M", t):
                    return
                wait_read(pool, work, ("M", "gu", k), t)
                wait_read(pool, work, ("M", "wb", k // 2), t)
                g.tensor_tensor(hid[:, 2 * k:2 * k + 2, :], su[:, 2 * k:2 * k + 2, :], wb[:, 2 * k:2 * k + 2, :], ALU.mult).then_inc(hid_ready, 1)

            def router_weights(t):
                if not has_row("M", t):
                    return
                r = row_of("M", t)
                done = 0

                def step(ins):
                    nonlocal done
                    done += 1
                    ins.then_inc(share_step, 1)
                    pool.wait_ge(share_step, SHARE_STEPS * r + done)

                pool.wait_ge(egap_ready, r + 1)
                pool.wait_ge(idx_ready, r + 1)
                detach(pool)
                step(g.tensor_scalar(den2[:], egap[:], 1.0, None, ALU.add))
                step(g.tensor_tensor(p12[:, 0:1], den2[:], minus_one[:], ALU.pow))
                step(g.tensor_tensor(p12[:, 1:2], p12[:, 0:1], egap[:], ALU.mult))
                detach(pool)
                step(g.tensor_scalar(w1st[:], expert[:], idxf[:, 0:1], p12[:, 0:1], ALU.is_equal, ALU.mult))
                detach(pool)
                step(g.tensor_scalar(w2nd[:], expert[:], idxf[:, 1:2], p12[:, 1:2], ALU.is_equal, ALU.mult))
                step(g.tensor_tensor(wtok[:], w1st[:], w2nd[:], ALU.add))
                detach(pool)
                step(g.tensor_copy(wexp[:, 0:E], wtok[:]))
                step(g.tensor_tensor(wres[:], wtok[:], wexp[:, 0:E], ALU.subtract))
                detach(pool)
                step(g.tensor_copy(wexp[:, E:2 * E], wres[:]))
                g.tensor_tensor(wexp[:, 2 * E:3 * E], wres[:], wexp[:, E:2 * E], ALU.subtract).then_inc(wexp_ready, 1)
                assert done == SHARE_STEPS

            def body(t):
                layernorm_rstd("P", t)
                if isinstance(t, int) and t == 0:
                    constants()
                    pool.wait_ge(zeroed_ready, N_ZEROED)
                router_weights(t)
                key_parts(t)
                for k in range(FT // 2):
                    hidden_weighed(t, k)
                layernorm_rstd("B", t)
                if has_row("B", t):
                    if isinstance(t, int):
                        pool.wait_ge(ld_ffn, LD_FFN)
                    g.tensor_tensor(xb[:], x3[:], bdn_sb[:], ALU.add).then_inc(xb_ready, 1)
                values(t)
                layernorm_rstd("M", t)
                layernorm_rstd("A", t)

            pipeline(pool, body)

        @block.scalar
        def _(act):
            a = nc.scalar
            act.dma_start(upa_sb[:], upa).then_inc(ld_lora, 16)
            act.dma_start(upb_sb[:], upb).then_inc(ld_lora, 16)
            act.dma_start(dna_sb[:], dna).then_inc(ld_lora, 16)
            act.dma_start(dnb_sb[:], dnb).then_inc(ld_lora, 16)

            def copy_lora(t, b):
                if isinstance(t, int) and t == LORA_BODY:
                    act.wait_ge(lora_mm, b + 1)
                    if b < N_LORA // 2:
                        a.activation(upw[:, b // 2, (b % 2) * 512:(b % 2 + 1) * 512], ps_lora[:], ACT.Copy).then_inc(lora_copied, 1)
                    else:
                        c = 2 * b - N_LORA
                        a.activation(dnw[:, c:c + 2, :], heads(ps_lora[:], D), ACT.Copy).then_inc(lora_copied, 1)

            def exps(s, t, k):
                if not has_row(s, t):
                    return
                key = (s, "s", k)
                n = far.before(key, t)
                act.wait_ge(far.full, n + 1)
                wait_at_least(act, pv_done, n - NPT + 1)
                a.activation(pt[far.order.index(key) % NPT][:], heads(ps_far[far.bank(key)][:], P), ACT.Exp,
                             scale=float(HD0 if s == "A" else HD1) ** -0.5).then_inc(exp_ready, 1)

            def copy_tiles(ring, key, dst, t):
                if has_row(key[0], t):
                    wait_full(act, ring, key, t)
                    a.activation(dst, heads(bank(ring, key)[:].bitcast(BF16), P), ACT.Copy).then_inc(read_sem(ring, key), 1)

            def transposed(ring, key, dst, t, n=DC):
                if has_row(key[0], t):
                    wait_full(act, ring, key, t)
                    a.activation(dst, heads(bank(ring, key)[:, 0:n * P], P), ACT.Copy).then_inc(read_sem(ring, key), 1)

            def keys_k(t):
                if has_row("K", t):
                    act.wait_ge(cinb_in, 16 * (row_of("K", t) + 1))
                    if has_row("B", t):
                        wait_full(act, work, ("B", "kt"), t)
                    a.activation(slots(kexp1, HD1)[:, :, 1:6:2, :], repeated(cinb[:], 3, HD1), ACT.Copy).then_inc(kh1_ready, 1)

            def keys_p(t):
                if has_row("P", t):
                    key = ("P", "kv")
                    wait_full(act, work, key, t)
                    kv = bank(work, key)
                    a.activation(slots(kexp0, HD0)[:, :, 1:6:2, :], repeated(kv[:, 0:D], 3, HD0), ACT.Copy).then_inc(kh0_ready, 1)
                    wait_at_least(act, ao_ready["A"], row_of("P", t))
                    a.activation(va0[:, :, 0:HD0], heads(kv[:, D:2 * D], HD0), ACT.Copy).then_inc(v0_ready, 1)

            def keys_p_middle(t):
                if has_row("P", t):
                    wait_read(act, work, ("P", "kv"), t)
                    a.activation(slots(kexp0, HD0)[:, :, 2:5:2, :], repeated(kres[:], 2, HD0), ACT.Copy).then_inc(km0_ready, 1)

            def queries_p(t):
                if has_row("P", t):
                    if isinstance(t, int) and t == 0:
                        act.wait_ge(zeroed_ready, N_ZEROED)
                    wait_full(act, work, ("P", "q"), t)
                    a.activation(slots(qexp0, HD0)[:, :, 0:3, :], repeated(bank(work, ("P", "q"))[:, 0:D], 3, HD0), ACT.Copy).then_inc(qh0_ready, 1)

            def queries_p_middle(t):
                if has_row("P", t):
                    wait_read(act, work, ("P", "q"), t)
                    a.activation(slots(qexp0, HD0)[:, :, 3:5, :], repeated(qres0[:], 2, HD0), ACT.Copy).then_inc(qm0_ready, 1)

            def queries_m(t):
                if has_row("M", t):
                    act.wait_ge(xhat_ready["M"], row_of("M", t) + 1)
                    a.activation(slots(qexp1, HD1)[:, :, 0:3, :], repeated(xhat["M"][:], 3, HD1), ACT.Copy).then_inc(qh1_ready, 1)

            def queries_m_middle(t):
                if has_row("M", t):
                    act.wait_ge(qres1_ready, row_of("M", t) + 1)
                    a.activation(slots(qexp1, HD1)[:, :, 3:5, :], repeated(qres1[:], 2, HD1), ACT.Copy).then_inc(qm1_ready, 1)

            def tanh(t, k):
                if has_row("M", t):
                    wait_full(act, work, ("M", "gu", k), t)
                    a.activation(th[:, 2 * k:2 * k + 2, :], heads(bank(work, ("M", "gu", k))[:, 0:2 * P], P), ACT.Tanh, scale=0.5).then_inc(th_ready, 1)

            def softmax_of_two(t):
                if has_row("M", t):
                    act.wait_ge(gap_ready, row_of("M", t) + 1)
                    a.activation(egap[:], gap[:], ACT.Exp).then_inc(egap_ready, 1)

            def relu(t, k):
                if has_row("F", t):
                    if isinstance(t, int):
                        act.wait_ge(ld_ffn, LD_FFN)
                    key = ("F", "up", k)
                    wait_full(act, work, key, t)
                    for n in range(4):
                        h = 4 * k + n
                        last = a.activation(hft[:, h, :], bank(work, key)[:, n * P:(n + 1) * P], ACT.Relu, bias=bup_sb[:, h:h + 1])
                    last.then_inc(read_sem(work, key), 1)

            def spread_weights(t, k):
                if has_row("M", t):
                    key = ("M", "wb", k)
                    n = 4 if k == 0 else FT - 4
                    wait_full(act, work, key, t)
                    a.activation(wb[:, 4 * k:4 * k + n, :], heads(bank(work, key)[:, 0:n * P], P), ACT.Copy).then_inc(read_sem(work, key), 1)

            def body(t):
                transposed(work, ("M", "xt"), xht1[:], t)
                copy_tiles(near, ("B", "qt", 1), qt1[:, 8:16, :], t)
                softmax_of_two(t)
                keys_k(t)
                tanh(t, 0)
                copy_lora(t, 0)
                keys_p(t)
                transposed(work, ("P", "xt"), xht0[:], t)
                keys_p_middle(t)
                copy_lora(t, 1)
                tanh(t, 1)
                queries_p(t)
                queries_p_middle(t)
                copy_lora(t, 2)
                copy_tiles(work, ("P", "kt", 1), kt0[:, 8:16, :], t)
                copy_lora(t, 3)
                tanh(t, 2)
                exps("B", t, 0)
                exps("B", t, 1)
                copy_tiles(work, ("P", "qt", 1), qt0[:, 8:16, :], t)
                copy_lora(t, 4)
                for k in range(2, 5):
                    exps("B", t, k)
                spread_weights(t, 0)
                exps("B", t, 5)
                spread_weights(t, 1)
                exps("B", t, 6)
                exps("B", t, 7)
                copy_lora(t, 5)
                exps("A", t, 0)
                exps("A", t, 1)
                exps("A", t, 2)
                transposed(work, ("F", "xt"), xht3[:], t)
                exps("A", t, 3)
                queries_m(t)
                relu(t, 0)
                queries_m_middle(t)
                copy_lora(t, 6)
                transposed(near, ("A", "at"), aot[:], t)
                relu(t, 1)
                copy_lora(t, 7)

            act.wait_ge(zeroed_ready, 2)
            pipeline(act, body)

        @block.vector
        def _(dve):
            v = nc.vector
            now, steps = {}, {}

            def done(s, ins):
                steps[s] += 1
                ins.then_inc(vstep[s], 1)
                dve.wait_ge(vstep[s], VSTEPS[s] * row_of(s, now["t"]) + steps[s])

            def stats_of(s, src):
                done(s, v.bn_stats(stats[s][:], src[:]))
                detach(dve)
                v.bn_aggr(mv[s][:], stats[s][:]).then_inc(ln_var[s], 1)

            def normalise(s, t, src):
                dve.wait_ge(ln_rstd[s], row_of(s, t) + 1)
                v.tensor_scalar(xhat[s][:], src[:], mv[s][:, 0:1], rstd[s][:], ALU.subtract, ALU.mult).then_inc(xhat_ready[s], 1)

            def copy_transposes(ring, key, dst, t):
                if has_row(key[0], t):
                    wait_full(dve, ring, key, t)
                    v.tensor_copy(dst, heads(bank(ring, key)[:].bitcast(BF16), P)).then_inc(read_sem(ring, key), 1)

            def maximum(s, t, k):
                if not has_row(s, t):
                    return
                key = (s, "nat", k)
                wait_full(dve, near, key, t)
                src = bank(near, key)[:]
                if s == "B":
                    u, j = k // 2, 2 * (k % 2)
                    src = src.rearrange("p (j g k) -> p j g k", j=2, g=2)
                    dst = nmax[s][:, j:j + 2, 2 * u:2 * u + 2]
                else:
                    src = src.rearrange("p (j k) -> p j k", j=4)
                    dst = nmax[s][:, :, k]
                v.tensor_reduce(dst, src, AX_X, ALU.max, negate=True).then_inc(read_sem(near, key), 1)

            def maximum_parts(s, t):
                if not has_row(s, t):
                    return
                groups = KV1 if s == "B" else N0
                for k in range(2):
                    wait_read(dve, near, (s, "nat", (N1 if s == "B" else N0) - 1 - k), t)
                m = mexp[s]
                r = row_of(s, t)
                v.tensor_copy(m[:, :, 0:groups], nmax[s][:, :, 0:groups]).then_inc(mhigh_ready[s], 1)
                dve.wait_ge(mhigh_ready[s], r + 1)
                v.tensor_tensor(m[:, :, KV1:KV1 + groups], nmax[s][:, :, 0:groups], m[:, :, 0:groups],
                                ALU.subtract).then_inc(mexp_ready[s], 1)

            def copy_maxima(s, t):
                if has_row(s, t):
                    key = (s, "mt")
                    wait_full(dve, near, key, t)
                    v.tensor_copy(mt[s][:], bank(near, key)[:, 0:2 * P].bitcast(BF16)).then_inc(read_sem(near, key), 1)

            def attended(s, t):
                nh, hd = (NH1, HD1) if s == "B" else (NH0, HD0)
                dve.wait_ge(pv_done, far.before((s, "s", nh // 4 - 1), t) + 1)
                o = ps_pv[s][:, 0:nh * (hd + 1)].rearrange("p (h d) -> p h d", d=hd + 1)
                r = rden[s][:, 0:nh].rearrange("p (h d) -> p h d", d=1)
                done(s, v.reciprocal(r, o[:, :, hd:hd + 1]))
                v.tensor_tensor(heads(ao[s][:], hd), o[:, :, 0:hd], r.broadcast_to([P, nh, hd]), ALU.mult).then_inc(ao_ready[s], 1)

            def norm_p(t):
                if has_row("P", t):
                    dve.wait_ge(x_in, 16 * (row_of("P", t) + 1))
                    stats_of("P", xin)

            def router(t):
                if not has_row("M", t):
                    return
                key = ("M", "rt")
                wait_full(dve, work, key, t)
                v.tensor_copy(score[:], bank(work, key)[:, 0:E]).then_inc(read_sem(work, key), 1)

            def top_two(t):
                if not has_row("M", t):
                    return
                wait_read(dve, work, ("M", "rt"), t)
                detach(dve)
                done("M", v.max(top8[:], score[:]))
                v.tensor_tensor(gap[:], top8[:, 1:2], top8[:, 0:1], ALU.subtract).then_inc(gap_ready, 1)
                detach(dve)
                done("M", v.max_index(idx8[:], top8[:], score[:]))
                v.tensor_copy(idxf[:], idx8[:, 0:2]).then_inc(idx_ready, 1)

            def hidden(t, k):
                if not has_row("M", t):
                    return
                key = ("M", "gu", k)
                n = (FT // 2) * row_of("M", t) + k + 1
                two = slice(2 * k, 2 * k + 2)
                dve.wait_ge(th_ready, n)
                v.scalar_tensor_tensor(sg[:, two, :], th[:, two, :], 1.0, heads(bank(work, key)[:, 0:2 * P], P), ALU.add, ALU.mult).then_inc(sg_ready, 1)
                dve.wait_ge(sg_ready, n)
                v.tensor_tensor(su[:, two, :], sg[:, two, :], heads(bank(work, key)[:, 2 * P:4 * P], P), ALU.mult).then_inc(read_sem(work, key), 1)

            def keys_p(t):
                if has_row("P", t):
                    key = ("P", "kv")
                    dve.wait_ge(kh0_ready, row_of("P", t) + 1)
                    dve.wait_ge(v0_ready, row_of("P", t) + 1)
                    v.tensor_tensor(heads(kres[:], HD0), heads(bank(work, key)[:, 0:D], HD0),
                                    slots(kexp0, HD0)[:, :, 1, :], ALU.subtract).then_inc(read_sem(work, key), 1)

            def low_part(s, t, exp, hd, res, slot, middle, ready):
                if has_row(s, t):
                    dve.wait_ge(middle, row_of(s, t) + 1)
                    x = slots(exp, hd)
                    v.tensor_tensor(x[:, :, slot, :], heads(res[:], hd), x[:, :, 4, :], ALU.subtract).then_inc(ready, 1)

            def queries_p(t):
                if has_row("P", t):
                    key = ("P", "q")
                    dve.wait_ge(qh0_ready, row_of("P", t) + 1)
                    v.tensor_tensor(heads(qres0[:], HD0), heads(bank(work, key)[:, 0:D], HD0), slots(qexp0, HD0)[:, :, 0, :],
                                    ALU.subtract).then_inc(read_sem(work, key), 1)

            def keys_b(t):
                if has_row("B", t):
                    key = ("B", "kt")
                    wait_full(dve, work, key, t)
                    tiles = heads(bank(work, key)[:, 0:2 * P].bitcast(BF16), P)
                    for half in range(2):
                        rows = slice(half * L, (half + 1) * L)
                        last = v.tensor_copy(kz1[rows, half::2, :], tiles[rows])
                    last.then_inc(read_sem(work, key), 1)

            def end_a(t):
                if has_row("A", t):
                    key = ("A", "out")
                    wait_full(dve, near, key, t)
                    dve.wait_ge(xres_in, 16 * (row_of("A", t) + 1))
                    v.tensor_tensor(x1[:], xres[:], bank(near, key)[:, 0:D], ALU.add).then_inc(read_sem(near, key), 1)
                    wait_read(dve, near, key, t)
                    stats_of("A", x1)

            def end_m(t):
                if not has_row("M", t):
                    return
                key = ("M", "dn")
                wait_full(dve, work, key, t)
                v.tensor_tensor(x2[:], x1[:], bank(work, key)[:, 0:D], ALU.add).then_inc(read_sem(work, key), 1)
                wait_read(dve, work, key, t)
                stats_of("M", x2)

            def norm_m(t):
                if not has_row("M", t):
                    return
                r = row_of("M", t)
                dve.wait_ge(ln_rstd["M"], r + 1)
                src = x2[:].rearrange("p (u g j d) -> p u g j d", u=KV1 // 2, g=2, j=G1)
                dst = xhat["M"][:].rearrange("p (u j g d) -> p u j g d", u=KV1 // 2, g=2, j=G1)
                for g in range(2):
                    last = v.tensor_scalar(dst[:, :, :, g, :], src[:, :, g, :, :], mv["M"][:, 0:1], rstd["M"][:], ALU.subtract, ALU.mult)
                last.then_inc(xhat_ready["M"], 1)
                dve.wait_ge(xhat_ready["M"], r + 1)
                dve.wait_ge(qh1_ready, r + 1)
                v.tensor_tensor(heads(qres1[:], HD1), heads(xhat["M"][:], HD1), slots(qexp1, HD1)[:, :, 0, :],
                                ALU.subtract).then_inc(qres1_ready, 1)

            def dequantise(t, at, w, q, s, step):
                if not isinstance(t, int) or t != at:
                    return
                if step == 0:
                    dve.wait_ge(ld_ffn, LD_FFN)
                    v.scalar_tensor_tensor(s[:], q[:], -7.5, s[:], ALU.add, ALU.mult).then_inc(deq_tmp, 1)
                else:
                    dve.wait_ge(deq_tmp, 2)
                    dve.wait_ge(lora_copied, N_LORA // 2 if w is upw else N_LORA)
                    v.tensor_tensor(w[:], w[:], s[:], ALU.add).then_inc(deq_ready, 1)

            def set_up():
                for t in [qexp0, mexp["A"], mexp["B"], kexp1, kz1, qexp1, wexp]:
                    v.memset(t[:], 0.0).then_inc(zeroed_ready, 1)
                v.memset(minus_one[:], -1.0).then_inc(zeroed_ready, 1)
                v.memset(va1[:], 1.0).then_inc(zeroed_ready, 1)
                for e in range(E):
                    v.memset(expert[:, e:e + 1], float(e)).then_inc(zeroed_ready, 1)

            v.memset(kexp0[:], 0.0).then_inc(zeroed_ready, 1)
            v.memset(va0[:], 1.0).then_inc(zeroed_ready, 1)

            def body(t):
                now["t"] = t
                steps.update({s: 0 for s in LAG})
                norm_p(t)
                keys_b(t)
                router(t)
                if has_row("P", t):
                    key = ("P", "ct")
                    wait_full(dve, work, key, t)
                    v.tensor_copy(ct[:], bank(work, key)[0:L, 0:P]).then_inc(read_sem(work, key), 1)
                copy_transposes(near, ("B", "qt", 0), qt1[:, 0:8, :], t)
                top_two(t)
                if has_row("P", t):
                    normalise("P", t, xin)
                if isinstance(t, int) and t == 0:
                    set_up()
                maximum("B", t, 0)
                hidden(t, 0)
                maximum("B", t, 1)
                keys_p(t)
                maximum("B", t, 2)
                maximum("B", t, 3)
                low_part("P", t, kexp0, HD0, kres, 0, km0_ready, kexp0_ready)
                dequantise(t, 1, dnw, dnq_sb, dns_sb, 0)
                maximum("B", t, 4)
                hidden(t, 1)
                queries_p(t)
                maximum("B", t, 5)
                copy_transposes(work, ("P", "kt", 0), kt0[:, 0:8, :], t)
                maximum("B", t, 6)
                low_part("P", t, qexp0, HD0, qres0, 5, qm0_ready, qexp0_ready)
                dequantise(t, 1, upw, upq_sb, ups_sb, 1)
                maximum("B", t, 7)
                maximum_parts("B", t)
                copy_maxima("B", t)
                if has_row("G", t):
                    r = row_of("G", t)
                    dve.wait_ge(down_full, r + 1)
                    dve.wait_ge(xb_ready, r + 1)
                    wait_at_least(dve, stored, 16 * r)
                    v.tensor_tensor(xo[:], xb[:], ps_pv["B"][:, 0:D], ALU.add).then_inc(xo_ready, 1)
                hidden(t, 2)
                copy_transposes(work, ("P", "qt", 0), qt0[:, 0:8, :], t)
                maximum("A", t, 0)
                if has_row("M", t):
                    key = ("M", "wt")
                    wait_full(dve, work, key, t)
                    v.tensor_copy(wt[:], bank(work, key)[:, 0:P // 2].bitcast(BF16)).then_inc(read_sem(work, key), 1)
                for k in range(1, N0):
                    maximum("A", t, k)
                maximum_parts("A", t)
                copy_maxima("A", t)
                dequantise(t, 0, upw, upq_sb, ups_sb, 0)
                dequantise(t, 2, dnw, dnq_sb, dns_sb, 1)
                if has_row("B", t):
                    attended("B", t)
                    r = row_of("B", t)
                    dve.wait_ge(ao_ready["B"], r + 1)
                    v.tensor_tensor(x3[:], x2[:], ao["B"][:], ALU.add).then_inc(x3_ready, 1)
                    dve.wait_ge(x3_ready, r + 1)
                    stats_of("B", x3)
                    normalise("B", t, x3)
                end_m(t)
                norm_m(t)
                low_part("M", t, qexp1, HD1, qres1, 5, qm1_ready, qexp1_ready)
                if has_row("A", t):
                    attended("A", t)
                end_a(t)
                if has_row("A", t):
                    normalise("A", t, x1)
                assert all(steps[s] == VSTEPS[s] for s in LAG if has_row(s, t)), steps

            pipeline(dve, body)

        @block.tensor
        def _(pe):
            m = nc.tensor

            def lora(t, b):
                if not isinstance(t, int) or t != LORA_BODY:
                    return
                if b == 0:
                    pe.wait_ge(ld_lora, 64)
                else:
                    pe.wait_ge(lora_copied, b)
                if b < N_LORA // 2:
                    m.matmul(ps_lora[:], upa_sb[:, (b // 2) * P:(b // 2 + 1) * P], upb_sb[:, (b % 2) * 512:(b % 2 + 1) * 512],
                             start=True, stop=True).then_inc(lora_mm, 1)
                else:
                    for n in range(2):
                        c = 2 * b - N_LORA + n
                        last = m.matmul(ps_lora[:, n * D:(n + 1) * D], dna_sb[:, c * P:(c + 1) * P], dnb_sb[:], start=True, stop=True)
                    last.then_inc(lora_mm, 1)

            def transpose_rows(ring, key, src, t, chunks):
                wait_free(pe, ring, key, t)
                for n, c in enumerate(chunks):
                    last = m.transpose(bank(ring, key)[:, n * P:(n + 1) * P], src[:, c * P:(c + 1) * P], idf[:])
                last.then_inc(ring.full, 1)

            def transpose_tiles(ring, key, tiles, t):
                wait_free(pe, ring, key, t)
                to = bank(ring, key)[:].bitcast(BF16)
                for k, tile in enumerate(tiles):
                    last = m.transpose(to[:, k * P:(k + 1) * P], tile, idb[:])
                last.then_inc(ring.full, 1)

            def product(ring, key, t, left, right, chunks, width=D):
                wait_free(pe, ring, key, t)
                for c in range(chunks):
                    last = m.matmul(bank(ring, key)[:, 0:width], left[:, c, :], right[:, c, :], start=c == 0, stop=c == chunks - 1)
                last.then_inc(ring.full, 1)

            def natural(s, t, k):
                if not has_row(s, t):
                    return
                key = (s, "nat", k)
                wait_free(pe, near, key, t)
                to = bank(near, key)
                if s == "B":
                    if k == 0:
                        wait_read(pe, work, ("B", "kt"), t)
                    if k % 4 == 0:
                        wait_read(pe, near, ("B", "qt", k // 4), t)
                    u = k // 2
                    for jj in range(2):
                        j = 2 * (k % 2) + jj
                        last = m.matmul(to[:, jj * 2 * P:(jj + 1) * 2 * P], qt1[:, 4 * u + j, :], kz1[:, 2 * u:2 * u + 2, :],
                                        start=True, stop=True)
                else:
                    if k == 0:
                        for n in range(2):
                            wait_read(pe, work, ("P", "kt", n), t)
                            wait_read(pe, work, ("P", "qt", n), t)
                    m.matmul(to[:], idb[:], maskq[:], start=True, stop=False, skip_group_check=True)
                    for j in range(4):
                        h = 4 * k + j
                        last = m.matmul(to[:, j * P:(j + 1) * P], qt0[:, h, :], kt0[:, h, :], start=False, stop=True,
                                        skip_group_check=True)
                last.then_inc(near.full, 1)

            def transpose_maxima(s, t):
                if has_row(s, t):
                    pe.wait_ge(mexp_ready[s], row_of(s, t) + 1)
                    transpose_tiles(near, (s, "mt"), [mexp[s][:, j, :] for j in range(G1)], t)

            def shifted(s, t, k):
                if not has_row(s, t):
                    return
                key = (s, "s", k)
                wait_at_least(pe, exp_ready, far.before(key, t) - 1)
                if k == 0:
                    wait_read(pe, near, (s, "mt"), t)
                to = ps_far[far.bank(key)]
                if s == "B":
                    m.matmul(to[:], selg[:, k, :], mt[s][:], start=True, stop=False)
                    last = m.matmul(to[:], kz1[:, k, :], qt1[:, 4 * (k // 2):4 * (k // 2) + 4, :], start=False, stop=True)
                else:
                    m.matmul(to[:], idb[:], maskk[:], start=True, stop=False, skip_group_check=True)
                    m.matmul(to[:], selg[:, k, :], mt[s][:], start=False, stop=False, skip_group_check=True)
                    for j in range(4):
                        h = 4 * k + j
                        last = m.matmul(to[:, j * P:(j + 1) * P], kt0[:, h, :], qt0[:, h, :], start=False, stop=True,
                                        skip_group_check=True)
                last.then_inc(far.full, 1)

            def weigh_values(s, t, k):
                if not has_row(s, t):
                    return
                key = (s, "s", k)
                r = row_of(s, t)
                pe.wait_ge(exp_ready, far.before(key, t) + 1)
                if k == 0:
                    if s == "B":
                        wait_at_least(pe, xo_ready, r)
                    else:
                        wait_at_least(pe, ao_ready[s], r)
                    pe.wait_ge(v1_ready if s == "B" else v0_ready, r + 1)
                w = (HD1 if s == "B" else HD0) + 1
                for j in range(4):
                    h = 4 * k + j
                    value = va1[:, k, :] if s == "B" else va0[:, h, :]
                    last = m.matmul(ps_pv[s][:, h * w:(h + 1) * w], pt[far.order.index(key) % NPT][:, j, :], value, start=True, stop=True)
                last.then_inc(pv_done, 1)

            def gate_up(t, k):
                if not has_row("M", t):
                    return
                key = ("M", "gu", k)
                if isinstance(t, int):
                    pe.wait_ge(ld_moe, 48)
                wait_free(pe, work, key, t)
                for n, w in enumerate((wg_sb, wu_sb)):
                    for tile in range(2):
                        f = 2 * k + tile
                        for c in range(DC):
                            last = m.matmul(bank(work, key)[:, (2 * n + tile) * P:(2 * n + tile + 1) * P], w[:, c, f * P:(f + 1) * P], xht1[:, c, :],
                                            start=c == 0, stop=c == DC - 1)
                last.then_inc(work.full, 1)

            def down(t, chunks):
                if not has_row("G", t):
                    return
                r = row_of("G", t)
                if 0 in chunks:
                    if isinstance(t, int):
                        pe.wait_ge(deq_ready, 2)
                    pe.wait_ge(ao_ready["B"], r + 1)
                for c in chunks:
                    if c % 4 == 0:
                        n = work.bank(("F", "up", c // 4))
                        pe.wait_ge(work.read[n], work.at_start(t, n))
                    last = m.matmul(ps_pv["B"][:, 0:D], hft[:, c, :], dnw[:, c, :], start=c == 0, stop=c == HT - 1, skip_group_check=True)
                if HT - 1 in chunks:
                    last.then_inc(down_full, 1)

            def up(t, k, tiles=range(4)):
                if not has_row("F", t):
                    return
                key = ("F", "up", k)
                if 0 in tiles:
                    wait_read(pe, work, ("F", "xt"), t)
                    if isinstance(t, int):
                        pe.wait_ge(deq_ready, 1)
                    wait_free(pe, work, key, t)
                for n in tiles:
                    h = 4 * k + n
                    for c in range(DC):
                        last = m.matmul(bank(work, key)[:, n * P:(n + 1) * P], upw[:, c, h * P:(h + 1) * P], xht3[:, c, :],
                                        start=c == 0, stop=c == DC - 1)
                if 3 in tiles:
                    last.then_inc(work.full, 1)

            def weights_spread(t, k):
                if not has_row("M", t):
                    return
                key = ("M", "wb", k)
                wait_read(pe, work, ("M", "wt"), t)
                wait_free(pe, work, key, t)
                sel = sele[:].rearrange("p e f -> p (e f)")
                for n in range(4 if k == 0 else FT - 4):
                    f = 4 * k + n
                    last = m.matmul(bank(work, key)[:, n * P:(n + 1) * P], sel[:, f * P:(f + 1) * P], wt[:], start=True, stop=True)
                last.then_inc(work.full, 1)

            def transpose_queries_p(t, c):
                if has_row("P", t):
                    pe.wait_ge(qexp0_ready, row_of("P", t) + 1)
                    transpose_tiles(work, ("P", "qt", c), [qexp0[:, 8 * c + k, :] for k in range(8)], t)

            def transpose_keys_p(t, c):
                if has_row("P", t):
                    pe.wait_ge(kexp0_ready, row_of("P", t) + 1)
                    transpose_tiles(work, ("P", "kt", c), [kexp0[:, 8 * c + k, :] for k in range(8)], t)

            def body(t):
                mm, b, a_, p_ = (has_row(s, t) for s in ("M", "B", "A", "P"))
                if a_:
                    down(t, range(4))
                if b:
                    pe.wait_ge(qexp1_ready, row_of("B", t) + 1)
                    for c in range(2):
                        transpose_tiles(near, ("B", "qt", c), [qexp1[:, 2 * k:2 * k + 2, :].rearrange("p h s -> p (h s)") for k in range(8 * c, 8 * c + 8)], t)
                if mm:
                    pe.wait_ge(xhat_ready["A"], row_of("M", t) + 1)
                    transpose_rows(work, ("M", "xt"), xhat["A"], t, range(DC))
                if b:
                    pe.wait_ge(kexp1_ready, row_of("B", t) + 1)
                    transpose_tiles(work, ("B", "kt"), [kexp1[:, 2 * u:2 * u + 2, :].rearrange("p g s -> p (g s)") for u in range(KV1 // 2)], t)
                if a_:
                    down(t, [4])
                if mm:
                    if isinstance(t, int):
                        pe.wait_ge(ld_moe, 48)
                    wait_read(pe, work, ("M", "xt"), t)
                    product(work, ("M", "rt"), t, xht1, wr_sb, DC, E)
                if p_:
                    key = ("P", "ct")
                    pe.wait_ge(c_in, 16 * (row_of("P", t) + 1))
                    wait_free(pe, work, key, t)
                    detach(pe)
                    m.transpose(bank(work, key)[0:L, 0:P], cin[:], idf[:]).then_inc(work.full, 1)
                lora(t, 0)
                gate_up(t, 0)
                natural("B", t, 0)
                natural("B", t, 1)
                if not a_:
                    down(t, range(5))
                if p_:
                    key = ("P", "kv")
                    if isinstance(t, int):
                        pe.wait_ge(ld_kv, 16)
                    wait_read(pe, work, ("P", "ct"), t)
                    wait_free(pe, work, key, t)
                    m.matmul(bank(work, key)[:], ct[:], wkv_sb[:], start=True, stop=True).then_inc(work.full, 1)
                down(t, [5])
                natural("B", t, 2)
                if p_:
                    pe.wait_ge(xhat_ready["P"], row_of("P", t) + 1)
                    transpose_rows(work, ("P", "xt"), xhat["P"], t, range(DC))
                lora(t, 1)
                down(t, [6])
                natural("B", t, 3)
                gate_up(t, 1)
                natural("B", t, 4)
                if p_:
                    if isinstance(t, int):
                        pe.wait_ge(ld_q, 16)
                    wait_read(pe, work, ("P", "xt"), t)
                    product(work, ("P", "q"), t, xht0, wq_sb, DC)
                lora(t, 2)
                natural("B", t, 5)
                natural("B", t, 6)
                down(t, [7])
                transpose_keys_p(t, 0)
                transpose_keys_p(t, 1)
                lora(t, 3)
                natural("B", t, 7)
                gate_up(t, 2)
                transpose_maxima("B", t)
                transpose_queries_p(t, 0)
                shifted("B", t, 0)
                shifted("B", t, 1)
                transpose_queries_p(t, 1)
                lora(t, 4)
                if isinstance(t, int) and t == 0:
                    pe.wait_ge(const_ready, N_CONST)
                for k in range(N0):
                    weigh_values("B", t, k)
                    shifted("B", t, k + 2)
                    natural("A", t, k)
                    if mm and k == 0:
                        pe.wait_ge(wexp_ready, row_of("M", t) + 1)
                        transpose_tiles(work, ("M", "wt"), [wexp[:]], t)
                    if k >= 2:
                        weights_spread(t, k - 2)
                lora(t, 5)
                weigh_values("B", t, 4)
                shifted("B", t, 6)
                weigh_values("B", t, 5)
                shifted("B", t, 7)
                transpose_maxima("A", t)
                weigh_values("B", t, 6)
                shifted("A", t, 0)
                weigh_values("B", t, 7)
                shifted("A", t, 1)
                weigh_values("A", t, 0)
                shifted("A", t, 2)
                if mm:
                    if isinstance(t, int):
                        pe.wait_ge(ld_down, 16)
                    pe.wait_ge(hid_ready, (FT // 2) * (row_of("M", t) + 1))
                    product(work, ("M", "dn"), t, hid, wd_sb, FT)
                if has_row("F", t):
                    pe.wait_ge(xhat_ready["B"], row_of("F", t) + 1)
                    transpose_rows(work, ("F", "xt"), xhat["B"], t, range(DC))
                weigh_values("A", t, 1)
                shifted("A", t, 3)
                up(t, 0)
                weigh_values("A", t, 2)
                weigh_values("A", t, 3)
                up(t, 1, range(3))
                lora(t, 6)
                if a_:
                    pe.wait_ge(ao_ready["A"], row_of("A", t) + 1)
                    transpose_rows(near, ("A", "at"), ao["A"], t, range(DC))
                up(t, 1, [3])
                if a_:
                    if isinstance(t, int):
                        pe.wait_ge(ld_out, 16)
                    wait_read(pe, near, ("A", "at"), t)
                    product(near, ("A", "out"), t, aot, wout_sb, DC)
                lora(t, 7)

            pe.wait_ge(ident_ready, 2)
            pipeline(pe, body)

    return nc


_INS = ["x", "ctx", "wq", "wkv", "wout", "wr", "wg", "wu", "wd", "upq", "ups", "bup", "upa", "upb", "dnq", "dns", "bdn", "dna", "dnb"]


def kernel(x, ctx_512, L0_xattn_Wq, L0_xattn_Wkv_expand, L0_xattn_Wout, L0_ffn_w_gate_router, L0_ffn_w_gate_proj,
           L0_ffn_w_up_proj, L0_ffn_w_down_proj, L1_ffn_w_up_q, L1_ffn_w_up_scale, L1_ffn_b_up, L1_ffn_w_up_lora_a,
           L1_ffn_w_up_lora_b, L1_ffn_w_down_q, L1_ffn_w_down_scale, L1_ffn_b_down, L1_ffn_w_down_lora_a, L1_ffn_w_down_lora_b):
    import numpy as np
    import concourse.bacc as bacc
    from concourse.bass_utils import run_bass_kernel_spmd

    laid = {
        "x": np.asarray(x), "ctx": np.asarray(ctx_512),
        "wq": np.asarray(L0_xattn_Wq).T, "wkv": np.asarray(L0_xattn_Wkv_expand).T, "wout": np.asarray(L0_xattn_Wout).T,
        "wr": np.asarray(L0_ffn_w_gate_router).T,
        "wg": np.asarray(L0_ffn_w_gate_proj).reshape(E * F, D).T, "wu": np.asarray(L0_ffn_w_up_proj).reshape(E * F, D).T,
        "wd": np.asarray(L0_ffn_w_down_proj).transpose(0, 2, 1).reshape(E * F, D),
        "upq": np.asarray(L1_ffn_w_up_q).T, "ups": np.asarray(L1_ffn_w_up_scale).T,
        "bup": np.asarray(L1_ffn_b_up).reshape(HT, P).T,
        "upa": np.asarray(L1_ffn_w_up_lora_a).T, "upb": np.asarray(L1_ffn_w_up_lora_b),
        "dnq": np.asarray(L1_ffn_w_down_q).T, "dns": np.asarray(L1_ffn_w_down_scale).T,
        "bdn": np.asarray(L1_ffn_b_down).reshape(1, D),
        "dna": np.asarray(L1_ffn_w_down_lora_a).T, "dnb": np.asarray(L1_ffn_w_down_lora_b),
    }
    nc = bacc.Bacc("TRN2", target_bir_lowering=False, num_devices=1)
    arrays, args = {}, []
    for name in _INS:
        a = np.ascontiguousarray(laid[name])
        arrays[f"in_{name}_dram"] = a
        args.append(nc.dram_tensor(f"in_{name}_dram", a.shape, mybir.dt.from_np(a.dtype), kind="ExternalInput").ap())
    out = nc.dram_tensor("out_dram", laid["x"].shape, F32, kind="ExternalOutput").ap()
    build(nc, *args, out)
    r = run_bass_kernel_spmd(nc, [arrays], core_ids=[0])
    return r.results[0]["out_dram"]
```
